# Optimizing a Trainium2 kernel written in Bass

```python
import numpy as np
import jax
import jax.numpy as jnp

def _softmax(x, axis=-1):
    return jax.nn.softmax(x, axis=axis)

def _gelu(x):
    return jax.nn.gelu(x, approximate=True)

def _silu(x):
    return jax.nn.silu(x)

def _sigmoid(x):
    return jax.nn.sigmoid(x)

def _layernorm(x, axis=-1, eps=1e-05):
    m = jnp.mean(x, axis=axis, keepdims=True)
    v = jnp.var(x, axis=axis, keepdims=True)
    return (x - m) / jnp.sqrt(v + eps)

def _scatter_add(tgt, idx, src, axis=0):
    return tgt.at[idx].add(src)

def _segment_sum(src, seg, n):
    return jax.ops.segment_sum(src, seg, n)
kernel_name = 'mk_xattn_ffn_d1_seqx_r8_839012'

def setup_inputs(seed: int=0):
    np.random.seed(seed)
    _w = jnp.asarray

    def _rec_inputs():
        import jax
        import jax.numpy as jnp
        _rk = jax.random.key(seed)
        x = 7.22e-05 + 1 * jax.random.normal(jax.random.fold_in(_rk, 1), (32, 128, 128), jnp.float32)
        _lenS = 128 - jax.random.randint(jax.random.fold_in(_rk, 7), (32,), 0, max(1, 128 // 4) + 1, jnp.int32)
        _lenS2 = 128 - jax.random.randint(jax.random.fold_in(_rk, 8), (32,), 0, max(1, 128 // 4) + 1, jnp.int32)
        _ctx_1024P = jax.random.normal(jax.random.fold_in(_rk, 11), (32, 16, 128), jnp.float32)
        _ctx_1024c = jax.random.dirichlet(jax.random.fold_in(_rk, 511), 0.3 * jnp.ones((16,), jnp.float32), (32, 128))
        _ctx_1024t = jnp.einsum('bsk,bkd->bsd', _ctx_1024c, _ctx_1024P)
        _ctx_1024t = _ctx_1024t * jax.lax.rsqrt(jnp.mean(jnp.square(_ctx_1024t)) + 1e-12) * 0.953939
        ctx_1024 = 4.13588e-05 + 0.999923 * (_ctx_1024t + 0.3 * jax.random.normal(jax.random.fold_in(_rk, 611), (32, 128, 128), jnp.float32))
        return (x, ctx_1024)
    x, ctx_1024 = _rec_inputs()

    def _L0_xattn_setup():
        import jax, jax.numpy as jnp
        import numpy as np
        H = 16

        def _forward(queries, keys, values, Wq, bq, Wk, bk, Wv, bv, Wo, bo):
            N, L, _ = queries.shape
            q = (queries @ Wq + bq).reshape(N, L, H, -1)
            k = (keys @ Wk + bk).reshape(N, L, H, -1)
            v = (values @ Wv + bv).reshape(N, L, H, -1)
            qp = jax.nn.elu(q) + 1.0
            kp = jax.nn.elu(k) + 1.0
            D = qp.shape[-1]
            K = v.shape[-1]

            def step(sums, inp):
                q_t, k_t, v_t = inp
                sums = sums + jnp.einsum('bhd,bhk->bhdk', k_t, v_t)
                out_t = jnp.einsum('bhdk,bhd->bhk', sums, q_t)
                return (sums, out_t)
            init = jnp.zeros((N, H, D, K), qp.dtype)
            xs = (jnp.swapaxes(qp, 0, 1), jnp.swapaxes(kp, 0, 1), jnp.swapaxes(v, 0, 1))
            _, res = jax.lax.scan(step, init, xs)
            res = jnp.swapaxes(res, 0, 1)
            Z = jnp.cumsum(qp, axis=1)
            out = (res / Z).reshape(N, L, -1)
            return out @ Wo + bo
        key = jax.random.key(seed)
        ks = jax.random.split(key, 8)
        N, L, dm = (4, 256, 128)
        scale = 0.02
        rn = lambda k, shape: jax.random.normal(k, shape, dtype=jnp.float32)
        return {'queries': rn(ks[0], (N, L, dm)), 'keys': rn(ks[1], (N, L, dm)), 'values': rn(ks[2], (N, L, dm)), 'Wq': rn(ks[3], (dm, dm)) * scale, 'bq': jnp.zeros((dm,), jnp.float32), 'Wk': rn(ks[4], (dm, dm)) * scale, 'bk': jnp.zeros((dm,), jnp.float32), 'Wv': rn(ks[5], (dm, dm)) * scale, 'bv': jnp.zeros((dm,), jnp.float32), 'Wo': rn(ks[6], (dm, dm)) * scale, 'bo': jnp.zeros((dm,), jnp.float32)}
    _L0_xattn_all = _L0_xattn_setup()
    _L0_xattn_in = {k: v for k, v in _L0_xattn_all.items() if k in ('Wq', 'bq', 'Wk', 'bk', 'Wv', 'bv', 'Wo', 'bo')}
    del _L0_xattn_all

    def _L0_ffn_setup():
        import jax, jax.numpy as jnp
        import numpy as np
        E, K = (8, 2)
        key = jax.random.key(seed)
        ks = jax.random.split(key, 5)
        B, S, H, I = (2, 128, 128, 512)
        scale_h = 1.0 / np.sqrt(H)
        scale_i = 1.0 / np.sqrt(I)
        return {'hidden_states': jax.random.normal(ks[0], (B, S, H), jnp.float32), 'conf_w': jax.random.normal(ks[1], (E, H), jnp.float32) * 0.1 * scale_h, 'conf_b': jnp.zeros((E,), jnp.float32), 'gate_w': jax.random.normal(ks[2], (E, I, H), jnp.float32) * scale_h, 'up_w': jax.random.normal(ks[3], (E, I, H), jnp.float32) * scale_h, 'down_w': jax.random.normal(ks[4], (E, H, I), jnp.float32) * scale_i, 'wealth': jnp.ones((E,), jnp.float32)}
    _L0_ffn_all = _L0_ffn_setup()
    _L0_ffn_in = {k: v for k, v in _L0_ffn_all.items() if k in ('conf_w', 'conf_b', 'gate_w', 'up_w', 'down_w', 'wealth')}
    del _L0_ffn_all
    return {'x': x, 'ctx_1024': ctx_1024, 'L0_xattn_Wq': _L0_xattn_in['Wq'], 'L0_xattn_bq': _L0_xattn_in['bq'], 'L0_xattn_Wk': _L0_xattn_in['Wk'], 'L0_xattn_bk': _L0_xattn_in['bk'], 'L0_xattn_Wv': _L0_xattn_in['Wv'], 'L0_xattn_bv': _L0_xattn_in['bv'], 'L0_xattn_Wo': _L0_xattn_in['Wo'], 'L0_xattn_bo': _L0_xattn_in['bo'], 'L0_ffn_conf_w': _L0_ffn_in['conf_w'], 'L0_ffn_conf_b': _L0_ffn_in['conf_b'], 'L0_ffn_gate_w': _L0_ffn_in['gate_w'], 'L0_ffn_up_w': _L0_ffn_in['up_w'], 'L0_ffn_down_w': _L0_ffn_in['down_w'], 'L0_ffn_wealth': _L0_ffn_in['wealth']}

def reference(x, ctx_1024, L0_xattn_Wq, L0_xattn_bq, L0_xattn_Wk, L0_xattn_bk, L0_xattn_Wv, L0_xattn_bv, L0_xattn_Wo, L0_xattn_bo, L0_ffn_conf_w, L0_ffn_conf_b, L0_ffn_gate_w, L0_ffn_up_w, L0_ffn_down_w, L0_ffn_wealth):
    import jax
    import jax.numpy as jnp

    def _L0_xattn_ref(queries, keys, values, Wq, bq, Wk, bk, Wv, bv, Wo, bo):
        import jax, jax.numpy as jnp
        import numpy as np
        H = 16

        def _forward(queries, keys, values, Wq, bq, Wk, bk, Wv, bv, Wo, bo):
            N, L, _ = queries.shape
            q = (queries @ Wq + bq).reshape(N, L, H, -1)
            k = (keys @ Wk + bk).reshape(N, L, H, -1)
            v = (values @ Wv + bv).reshape(N, L, H, -1)
            qp = jax.nn.elu(q) + 1.0
            kp = jax.nn.elu(k) + 1.0
            D = qp.shape[-1]
            K = v.shape[-1]

            def step(sums, inp):
                q_t, k_t, v_t = inp
                sums = sums + jnp.einsum('bhd,bhk->bhdk', k_t, v_t)
                out_t = jnp.einsum('bhdk,bhd->bhk', sums, q_t)
                return (sums, out_t)
            init = jnp.zeros((N, H, D, K), qp.dtype)
            xs = (jnp.swapaxes(qp, 0, 1), jnp.swapaxes(kp, 0, 1), jnp.swapaxes(v, 0, 1))
            _, res = jax.lax.scan(step, init, xs)
            res = jnp.swapaxes(res, 0, 1)
            Z = jnp.cumsum(qp, axis=1)
            out = (res / Z).reshape(N, L, -1)
            return out @ Wo + bo
        return _forward(queries, keys, values, Wq, bq, Wk, bk, Wv, bv, Wo, bo)

    def _L0_ffn_ref(hidden_states, conf_w, conf_b, gate_w, up_w, down_w, wealth):
        import jax, jax.numpy as jnp
        import numpy as np
        E, K = (8, 2)
        x = hidden_states
        confidences = jax.nn.sigmoid(jnp.einsum('bsh,eh->bse', x, conf_w) + conf_b)
        bids = confidences * wealth
        top_bids, selected_experts = jax.lax.top_k(bids, K)
        sorted_bids = -jnp.sort(-bids, axis=-1)
        payments = jnp.broadcast_to(sorted_bids[..., K:K + 1], top_bids.shape)
        routing_weights = jax.nn.softmax(top_bids, axis=-1)
        combine = jnp.sum(jax.nn.one_hot(selected_experts, E, dtype=x.dtype) * routing_weights[..., None], axis=2)

        def ffn(gw, uw, dw):
            g = jnp.einsum('bsh,ih->bsi', x, gw)
            u = jnp.einsum('bsh,ih->bsi', x, uw)
            return jnp.einsum('bsi,hi->bsh', jax.nn.silu(g) * u, dw)
        expert_out = jax.vmap(ffn)(gate_w, up_w, down_w)
        output = jnp.einsum('ebsh,bse->bsh', expert_out, combine)
        return output
    x = x + _L0_xattn_ref(_layernorm(x, axis=-1), ctx_1024, ctx_1024, L0_xattn_Wq, L0_xattn_bq, L0_xattn_Wk, L0_xattn_bk, L0_xattn_Wv, L0_xattn_bv, L0_xattn_Wo, L0_xattn_bo)
    x = x + _L0_ffn_ref(_layernorm(x, axis=-1), L0_ffn_conf_w, L0_ffn_conf_b, L0_ffn_gate_w, L0_ffn_up_w, L0_ffn_down_w, L0_ffn_wealth)
    return x

_drawn_inputs = setup_inputs


def setup_inputs(seed=0):
    import zlib

    import numpy as np

    out = dict(_drawn_inputs(seed))
    spreads = {'L0_xattn_bq': (0.0, 0.1),
     'L0_xattn_bk': (0.0, 0.608),
     'L0_xattn_bv': (0.0, 0.1),
     'L0_xattn_bo': (0.0, 0.1),
     'L0_ffn_conf_b': (0.0, 0.1),
     'L0_ffn_wealth': (1.0, 0.2)}
    factors = {'L0_xattn_Wk': 3.177}
    for name, (base, spread) in spreads.items():
        noise = np.random.default_rng([zlib.crc32(name.encode()), seed]).standard_normal(out[name].shape)
        drawn = base * np.exp(spread * noise) if base else spread * noise
        out[name] = jnp.asarray(drawn.astype(out[name].dtype))
    for name, factor in factors.items():
        out[name] = (out[name] * factor).astype(out[name].dtype)
    return out
```

```python
from contextlib import ExitStack

import concourse.bass as bass
from concourse import mybir

ALU = mybir.AluOpType
ACT = mybir.ActivationFunctionType
AX_X = mybir.AxisListType.X
F32 = mybir.dt.float32
F16 = mybir.dt.float16
U32 = mybir.dt.uint32

P = 128
WSCALE = 64.0
EPS = 1e-5


def attention_moe_kernel(nc, x, ctx_in, Wq, bq, Wk, bk, Wv, bv, Wo, bo,
                         conf_w, conf_b, gate_w, up_w, down_w, wealth, out):
    NB, L, D = x.shape
    E, I, _ = gate_w.shape
    H, HD = 16, D // 16
    UB = 4
    UNITS = NB // UB
    UT = UB * L
    CH = 64
    NCH = UB * L // CH
    RG = 4
    NBLK = 2 * RG
    IC = I // P
    assert L == P and D == P and E == UNITS and HD == 8 and L == 2 * CH

    with ExitStack() as ctx:
        def sb(name, shape, dt=F32):
            return ctx.enter_context(nc.sbuf_tensor(name, shape, dt))

        def sem(name):
            return ctx.enter_context(nc.semaphore(name))

        ident = sb("ident", [P, P])
        causal = sb("causal", [P, CH])
        headmask = sb("headmask", [P, 4])
        headsel = sb("headsel", [P, RG, 4])
        blockdiag = sb("blockdiag", [P, P])
        ones = sb("ones", [P, P])
        minus_half = sb("minus_half", [P, UB])
        eps = sb("eps", [P, UB])
        carrier = sb("carrier", [P, 1])
        iota8 = sb("iota8", [P, E])
        Wq_s, Wk_s, Wv_s, Wo_s = (sb(n, [P, P]) for n in ("Wq_s", "Wk_s", "Wv_s", "Wo_s"))
        bq_c, bk_c = sb("bq_c", [P, 1]), sb("bk_c", [P, 1])
        bq_neg, bk_neg = sb("bq_neg", [P, 1]), sb("bk_neg", [P, 1])
        bq_one, bk_one = sb("bq_one", [P, 1]), sb("bk_one", [P, 1])
        bv_b, bo_b = sb("bv_b", [P, P]), sb("bo_b", [P, P])
        cb_b, wealth_b = sb("cb_b", [P, E]), sb("wealth_b", [P, E])
        conf_s = sb("conf_s", [E, P])
        confT = sb("confT", [P, E])
        x_all = sb("x_all", [P, NB, P])
        ctx_s = [sb(f"ctx_s{i}", [P, UB, P]) for i in range(2)]
        stats1 = sb("stats1", [P, UB, 6])
        mv1 = sb("mv1", [P, UB, 2])
        ve1 = sb("ve1", [P, UB])
        rstd1 = sb("rstd1", [P, UB])
        xhat = sb("xhat", [P, UB, P])
        xT = sb("xT", [P, UT])
        cT = sb("cT", [P, NCH, 2, CH])
        neg = sb("neg", [P, 2, UT])
        expn = sb("expn", [P, 2, UT])
        qT = [sb(f"qT{i}", [P, UT]) for i in range(2)]
        kT = sb("kT", [P, UT])
        Kexp = [sb(f"Kexp{i}", [P, NCH, 4, CH]) for i in range(2)]
        Vexp = [sb(f"Vexp{i}", [P, NCH, RG, 2, 32]) for i in range(2)]
        Vtok = sb("Vtok", [CH, UB, P])
        Ktok = sb("Ktok", [CH, UB, P])
        state = [sb(f"state{i}", [P, UB, P]) for i in range(2)]
        Z = sb("Z", [P, UT])
        rZ = [sb(f"rZ{i}", [P, UT]) for i in range(2)]
        Pm = sb("Pm", [P, 4, UT])
        oT = sb("oT", [P, UT])
        stats2 = sb("stats2", [P, UB, 6])
        mv2 = sb("mv2", [P, UB, 2])
        ve2 = sb("ve2", [P, UB])
        rstd2 = sb("rstd2", [P, UB])
        x2hat = sb("x2hat", [P, UB, P])
        x2T = sb("x2T", [P, UT])
        x2hi = sb("x2hi", [P, NB * L], F16)
        x2lo = sb("x2lo", [P, NB * L], F16)
        conf = sb("conf", [P, UB, E])
        conf_e = sb("conf_e", [P, UB, E])
        bids = sb("bids", [P, UB, E])
        top = sb("top", [P, UB, 8])
        topi = sb("topi", [P, UB, 8], U32)
        vdiff = sb("vdiff", [P, UB])
        vexp = sb("vexp", [P, UB])
        wts = sb("wts", [P, 2, UB])
        hot = sb("hot", [P, 2, UB, E])
        comb = sb("comb", [P, NB, E])
        w_raw = [sb(f"w_raw{i}", [P, 3, IC * P]) for i in range(2)]
        w_hi = sb("w_hi", [P, E * 3 * IC * P], F16)
        w_lo = sb("w_lo", [P, E * 3 * IC * P], F16)
        silu = sb("silu", [P, 2, UT])
        hid = sb("hid", [P, 2, UT])
        hid_hi = sb("hid_hi", [P, 2, UT], F16)
        hid_lo = sb("hid_lo", [P, 2, UT], F16)

        bank = [ctx.enter_context(nc.psum_tensor(f"bank{i}", [P, 512], F32)) for i in range(8)]

        const_loaded = sem("const_loaded")
        const_made = sem("const_made")
        const_dve = sem("const_dve")
        confT_ps = sem("confT_ps")
        x_loaded = [sem(f"x_loaded{i}") for i in range(2)]
        ctx_loaded = [sem(f"ctx_loaded{i}") for i in range(2)]
        w_loaded = [sem(f"w_loaded{i}") for i in range(2)]
        stats1_done = sem("stats1_done")
        mv1_done = sem("mv1_done")
        ve1_done = sem("ve1_done")
        rstd1_done = sem("rstd1_done")
        xhat_done = sem("xhat_done")
        xb_done = sem("xb_done")
        xT_ps = sem("xT_ps")
        cT_ps = sem("cT_ps")
        xT_copied = sem("xT_copied")
        cT_copied = sem("cT_copied")
        q_ps = sem("q_ps")
        k_ps = sem("k_ps")
        v_ps = sem("v_ps")
        neg_done = sem("neg_done")
        exp_done = sem("exp_done")
        qk_done = sem("qk_done")
        kexp_done = sem("kexp_done")
        vexp_done = sem("vexp_done")
        ktok_ps = sem("ktok_ps")
        ktok_copied = sem("ktok_copied")
        state_ps = sem("state_ps")
        state_done = sem("state_done")
        z_done = sem("z_done")
        rz_done = sem("rz_done")
        scores_ps = sem("scores_ps")
        p_done = sem("p_done")
        av_done = sem("av_done")
        o_done = sem("o_done")
        ao_ps = sem("ao_ps")
        x1_done = sem("x1_done")
        stats2_done = sem("stats2_done")
        mv2_done = sem("mv2_done")
        ve2_done = sem("ve2_done")
        rstd2_done = sem("rstd2_done")
        x2hat_done = sem("x2hat_done")
        x2T_ps = sem("x2T_ps")
        x2T_copied = sem("x2T_copied")
        x2hi_done = sem("x2hi_done")
        x2lo_done = sem("x2lo_done")
        lg_ps = sem("lg_ps")
        lg_done = sem("lg_done")
        lg_exp = sem("lg_exp")
        router = sem("router")
        top_done = sem("top_done")
        vdiff_done = sem("vdiff_done")
        vexp_act = sem("vexp_act")
        w_ps = sem("w_ps")
        whi_done = sem("whi_done")
        wlo_done = sem("wlo_done")
        gu_ps = sem("gu_ps")
        silu_done = sem("silu_done")
        hid_done = sem("hid_done")
        hi_done = sem("hi_done")
        lo_done = sem("lo_done")
        hid_used = sem("hid_used")
        y_ps = sem("y_ps")
        acc_done = sem("acc_done")
        stored = sem("stored")

        block = ctx.enter_context(nc.Block())

        x_tok = x.rearrange("b t d -> t b d")
        ctx_tok = ctx_in.rearrange("b t d -> t b d")
        out_tok = out.rearrange("b t d -> t b d")
        N_MADE = 13

        def steady(run):
            run(0, 0)
            with run.engine.Fori(0, (UNITS - 2) // 2) as i:
                run(i * 2 + 1, 1)
                run(i * 2 + 2, 0)
            run(UNITS - 1, (UNITS - 1) % 2)

        class Units:

            def __init__(self, engine, body):
                self.engine, self.body = engine, body

            def __call__(self, u, par):
                self.body(u, par)

        def first(u):
            return isinstance(u, int) and u == 0

        def last(u):
            return isinstance(u, int) and u == UNITS - 1

        @block.sync
        def _(sp):
            def load_unit(u, par):
                if not (isinstance(u, int) and u < 2):
                    sp.wait_ge(x_loaded[par], 16 * ((u - par) // 2) if isinstance(u, int) else 16 * (u // 2))
                sp.dma_start(x_all[:, bass.ds(u * UB, UB), :], x_tok[:, bass.ds(u * UB, UB), :]).then_inc(x_loaded[par], 16)
                if not (isinstance(u, int) and u < 2):
                    sp.wait_ge(cT_ps, u - 1)
                sp.dma_start(ctx_s[par][:], ctx_tok[:, bass.ds(u * UB, UB), :]).then_inc(ctx_loaded[par], 16)

            def load_w(u, par):
                if not (isinstance(u, int) and u < 2):
                    sp.wait_ge(w_ps, 3 * (u - 1))
                for m, w in enumerate((gate_w, up_w)):
                    sp.dma_start(w_raw[par][:, m, :].rearrange("p (c h) -> p c h", c=IC),
                                 w[bass.ds(u, 1), :, :].rearrange("o (c p) h -> p (o c) h", p=P)).then_inc(w_loaded[par], 16)
                sp.dma_start(w_raw[par][:, 2, :],
                             down_w[bass.ds(u, 1), :, :].rearrange("o h i -> h (o i)")).then_inc(w_loaded[par], 16)

            load_unit(0, 0)
            for dst, src in ((Wq_s, Wq), (Wk_s, Wk), (Wv_s, Wv), (Wo_s, Wo), (conf_s, conf_w)):
                sp.dma_start(dst[:], src).then_inc(const_loaded, 16)
            for dst, src in ((bv_b, bv), (bo_b, bo), (cb_b, conf_b), (wealth_b, wealth)):
                sp.dma_start(dst[:], src.partition_broadcast(P)).then_inc(const_loaded, 16)
            for dst, src in ((bq_c, bq), (bk_c, bk)):
                sp.dma_start(dst[:], src.unsqueeze(1)).then_inc(const_loaded, 16)
            load_w(0, 0)
            load_unit(1, 1)
            load_w(1, 1)
            with sp.Fori(0, (UNITS - 2) // 2) as i:
                for par in range(2):
                    load_unit(i * 2 + 2 + par, par)
                    load_w(i * 2 + 2 + par, par)
            with sp.Fori(0, UNITS) as g:
                sp.wait_ge(acc_done, (E - 1) * UNITS * UB + UB * (g + 1))
                sp.dma_start(out_tok[:, bass.ds(g * UB, UB), :], x_all[:, bass.ds(g * UB, UB), :]).then_inc(stored, 16)
            sp.wait_ge(stored, 16 * UNITS)

        N_LOADS = 11

        @block.gpsimd
        def _(pool):
            n_made = [0]

            def made(ins):
                ins.then_inc(const_made, 1)
                n_made[0] += 1
                pool.wait_ge(const_made, n_made[0])

            made(pool.memset(ones[:], 1.0))
            made(pool.memset(minus_half[:], -0.5))
            made(pool.memset(eps[:], EPS))
            for i in range(2):
                made(pool.memset(Vexp[i][:], 0.0))
            made(pool.affine_select(ident[:], ones[:], [[1, P]], ALU.is_equal, 0.0, base=0, channel_multiplier=-1))
            for half in range(2):
                rows = slice(half * CH, half * CH + CH)
                made(pool.affine_select(causal[rows, :], ones[rows, 0:CH], [[1, CH]], ALU.is_ge, 0.0, base=0, channel_multiplier=-1))
            ones_h = ones[:, 0:H].rearrange("p (r j) -> p r j", r=RG)
            made(pool.affine_select(headsel[:], ones_h, [[-4 * HD, RG], [-HD, 4]], ALU.is_ge, 0.0, base=0, channel_multiplier=1))
            made(pool.affine_select(headsel[:], headsel[:], [[4 * HD, RG], [HD, 4]], ALU.is_ge, 0.0, base=HD - 1, channel_multiplier=-1))
            bd = blockdiag[:].rearrange("p (h k) -> p h k", h=H)
            made(pool.affine_select(bd, ones[:].rearrange("p (h k) -> p h k", h=H), [[-HD, H], [0, HD]], ALU.is_ge, 0.0, base=0, channel_multiplier=1))
            made(pool.affine_select(bd, bd, [[HD, H], [0, HD]], ALU.is_ge, 0.0, base=HD - 1, channel_multiplier=-1))
            made(pool.iota(iota8[:], [[1, E]], base=0, channel_multiplier=0, allow_small_or_imprecise_dtypes=True))
            pool.wait_ge(const_loaded, 16 * N_LOADS)

            def rstd(mv_done, mv, ve, ve_done, rs, rs_done, u):
                pool.wait_ge(mv_done, UB * (u + 1))
                pool.tensor_tensor(ve[:], mv[:, :, 1], eps[:], ALU.add).then_inc(ve_done, 1)
                pool.wait_ge(ve_done, u + 1)
                pool.tensor_tensor(rs[:], ve[:], minus_half[:], ALU.pow).then_inc(rs_done, 1)

            def front(u):
                rstd(mv1_done, mv1, ve1, ve1_done, rstd1, rstd1_done, u)
                pool.wait_ge(xhat_done, UB * (u + 1))
                xu = x_all[:, bass.ds(u * UB, UB), :]
                pool.tensor_tensor(xu, xu, bo_b[:].unsqueeze(1).to_broadcast([P, UB, P]), ALU.add).then_inc(xb_done, 1)

            def tail(u):
                rstd(mv2_done, mv2, ve2, ve2_done, rstd2, rstd2_done, u)

            def body(u, par):
                if not last(u):
                    front(u + 1)
                if not first(u):
                    tail(u - 1)

            front(0)
            steady(Units(pool, body))
            tail(UNITS - 1)

            with pool.Fori(0, E * UNITS) as n:
                for c in range(IC):
                    pool.wait_ge(hi_done, IC * n + c + 1)
                    pool.tensor_tensor(hid_lo[:, c % 2, :], hid[:, c % 2, :], hid_hi[:, c % 2, :], ALU.subtract).then_inc(lo_done, 1)

        @block.scalar
        def _(act):
            def weights(u, m):
                act.wait_ge(w_ps, 3 * u + m + 1)
                act.activation(w_hi[:, bass.ds(u * (3 * I) + m * I, I)], bank[2 + m % 2][:], ACT.Copy, scale=WSCALE).then_inc(whi_done, 1)

            def front_copies(u, par):
                act.wait_ge(xT_ps, u + 1)
                act.activation(xT[:], bank[0][:], ACT.Copy).then_inc(xT_copied, 1)
                act.wait_ge(cT_ps, u + 1)
                if not first(u):
                    act.wait_ge(v_ps, u)
                act.activation(cT[:], bank[1][:].rearrange("p (c s) -> p c s", s=CH).unsqueeze(2).to_broadcast([P, NCH, 2, CH]),
                               ACT.Copy).then_inc(cT_copied, 1)

            def front_exp(u, par):
                for m, (ps, ready, bneg) in enumerate(((bank[0], q_ps, bq_neg), (bank[1], k_ps, bk_neg))):
                    act.wait_ge(ready, u + 1)
                    act.activation(neg[:, m, :], ps[:], ACT.Relu, bias=bneg[:], scale=-1.0).then_inc(neg_done, 1)
                    act.wait_ge(neg_done, 2 * u + m + 1)
                    act.activation(expn[:, m, :], neg[:, m, :], ACT.Exp, scale=-1.0).then_inc(exp_done, 1)

            def front_ktok(u, par):
                act.wait_ge(ktok_ps, u + 1)
                act.activation(Ktok[:].rearrange("p b d -> p (b d)"), bank[0][0:CH, :], ACT.Copy).then_inc(ktok_copied, 1)

            def tail_x2(u):
                act.wait_ge(x2T_ps, u + 1)
                act.activation(x2T[:], bank[7][:], ACT.Copy).then_inc(x2T_copied, 1)
                act.activation(x2hi[:, bass.ds(u * UT, UT)], bank[7][:], ACT.Copy).then_inc(x2hi_done, 1)

            def tail_router(u):
                act.wait_ge(lg_done, u + 1)
                act.activation(conf_e[:], conf[:], ACT.Exp, scale=-1.0).then_inc(lg_exp, 1)
                act.wait_ge(vdiff_done, u + 1)
                act.activation(vexp[:], vdiff[:], ACT.Exp).then_inc(vexp_act, 1)

            def body(u, par):
                weights(u, 0)
                weights(u, 1)
                weights(u, 2)
                if not last(u):
                    front_copies(u + 1, 1 - par)
                    front_exp(u + 1, 1 - par)
                if not first(u):
                    tail_x2(u - 1)
                if not last(u):
                    front_ktok(u + 1, 1 - par)
                if not first(u):
                    tail_router(u - 1)

            act.wait_ge(const_dve, 6)
            front_copies(0, 0)
            front_exp(0, 0)
            front_ktok(0, 0)
            steady(Units(act, body))
            tail_x2(UNITS - 1)
            tail_router(UNITS - 1)

            with act.Fori(0, E * UNITS) as n:
                for c in range(IC):
                    act.wait_ge(gu_ps, IC * n + c + 1)
                    act.activation(silu[:, c % 2, :], bank[c % 2][:], ACT.Silu, scale=1.0 / WSCALE).then_inc(silu_done, 1)
                    act.wait_ge(hid_done, IC * n + c + 1)
                    act.activation(hid_hi[:, c % 2, :], hid[:, c % 2, :], ACT.Copy).then_inc(hi_done, 1)

        @block.vector
        def _(dve):
            def stats(u, st, st_done):
                for b in range(UB):
                    dve.bn_stats(st[:, b, :], x_all[:, bass.ds(u * UB + b, 1), :].rearrange("p o d -> p (o d)")).then_inc(st_done, 1)

            def aggregate(mv, st, mv_done):
                for b in range(UB):
                    dve.bn_aggr(mv[:, b, :], st[:, b, :]).then_inc(mv_done, 1)

            def wait_x(u, par):
                dve.wait_ge(x_loaded[par], 16 * (u // 2) + 16)

            def wait_stats1(u):
                dve.wait_ge(stats1_done, UB * (u + 1))

            def wait_x1(u):
                dve.wait_ge(x1_done, u + 1)

            def wait_stats2(u):
                dve.wait_ge(stats2_done, UB * (u + 1))

            def front_stats(u, par):
                stats(u, stats1, stats1_done)

            def front_norm(u, par):
                dve.wait_ge(rstd1_done, u + 1)
                if not first(u):
                    dve.wait_ge(xT_ps, u)
                for b in range(UB):
                    dve.tensor_scalar(xhat[:, b, :], x_all[:, bass.ds(u * UB + b, 1), :].rearrange("p o d -> p (o d)"),
                                      mv1[:, b, 0:1], rstd1[:, b:b + 1], ALU.subtract, ALU.mult).then_inc(xhat_done, 1)

            def front_qk(u, par):
                for m, (ps, dst, bone) in enumerate(((bank[0], qT[par], bq_one), (bank[1], kT, bk_one))):
                    dve.wait_ge(exp_done, 2 * u + m + 1)
                    dve.scalar_tensor_tensor(dst[:], ps[:], bone[:], expn[:, m, :], ALU.add, ALU.max).then_inc(qk_done, 1)
                dve.wait_ge(qk_done, 2 * u + 2)
                kv = kT[:].rearrange("p (c s) -> p c s", s=CH)
                for j in range(4):
                    dve.tensor_scalar(Kexp[par][:, :, j, :], kv, headmask[:, j:j + 1], None, ALU.mult).then_inc(kexp_done, 1)

            def front_v(u, par):
                dve.wait_ge(v_ps, u + 1)
                for half in range(2):
                    ps = bank[2 + half]
                    for a in range(2):
                        rows = slice(a * CH, a * CH + CH)
                        cs = slice(half * NCH // 2, (half + 1) * NCH // 2)
                        src = ps[rows, :].rearrange("p (x j a k) -> p x j a k", j=2, a=2, k=HD)[:, :, :, a, :]
                        dst = Vexp[par][rows, cs].rearrange("p c r j (i a k) -> p (c r) j i a k", i=2, a=2)
                        for j in range(2):
                            bvv = bv_b[rows, :].rearrange("p (r j a k) -> p r j a k", r=RG, j=2, a=2)[:, :, j, a, :]
                            dve.tensor_tensor(
                                dst[:, :, j, j, a, :].rearrange("p (c r) k -> p c r k", r=RG),
                                src[:, :, j, :].rearrange("p (c r) k -> p c r k", r=RG),
                                bvv.unsqueeze(1).to_broadcast([CH, NCH // 2, RG, HD]), ALU.add).then_inc(vexp_done, 1)
                    dve.tensor_tensor(Vtok[:, 2 * half:2 * half + 2, :],
                                      ps[0:CH, :].rearrange("p (b c k) -> p b c k", b=2, c=2)[:, :, 0, :],
                                      bv_b[0:CH, :].unsqueeze(1).to_broadcast([CH, 2, P]), ALU.add).then_inc(vexp_done, 1)

            def front_z(u, par):
                for b in range(UB):
                    cols = slice(b * L, (b + 1) * L)
                    dve.tensor_tensor_scan(Z[:, cols], ones[:], qT[par][:, cols], 0.0, ALU.mult, ALU.add).then_inc(z_done, 1)
                dve.wait_ge(z_done, UB * (u + 1))
                dve.reciprocal(rZ[par][:], Z[:]).then_inc(rz_done, 1)

            def front_state(u, par):
                dve.wait_ge(state_ps, u + 1)
                dve.tensor_tensor(state[par][:], bank[1][:].rearrange("p (b k) -> p b k", b=UB),
                                  blockdiag[:].unsqueeze(1).to_broadcast([P, UB, P]), ALU.mult).then_inc(state_done, 1)

            def mask_scores(u, t):
                dve.wait_ge(scores_ps, NBLK * u + t + 1)
                if t >= 4:
                    dve.wait_ge(av_done, NBLK * u + t - 3)
                dve.tensor_tensor(Pm[:, t % 4, :].rearrange("p (n t) -> p n t", t=CH),
                                  bank[4 + t % 2][:].rearrange("p (n t) -> p n t", t=CH),
                                  causal[:].unsqueeze(1).to_broadcast([P, UT // CH, CH]), ALU.mult).then_inc(p_done, 1)

            def tail_o(u, par):
                dve.wait_ge(av_done, NBLK * (u + 1))
                dve.wait_ge(rz_done, u + 1)
                dve.tensor_tensor(oT[:], bank[6][:], rZ[par][:], ALU.mult).then_inc(o_done, 1)

            def tail_x1(u):
                dve.wait_ge(ao_ps, u + 1)
                dve.wait_ge(xb_done, u + 1)
                xu = x_all[:, bass.ds(u * UB, UB), :]
                dve.tensor_tensor(xu, bank[7][:].rearrange("p (b d) -> p b d", b=UB), xu, ALU.add).then_inc(x1_done, 1)

            def tail_norm(u):
                dve.wait_ge(rstd2_done, u + 1)
                for b in range(UB):
                    dve.tensor_scalar(x2hat[:, b, :], x_all[:, bass.ds(u * UB + b, 1), :].rearrange("p o d -> p (o d)"),
                                      mv2[:, b, 0:1], rstd2[:, b:b + 1], ALU.subtract, ALU.mult).then_inc(x2hat_done, 1)

            def tail_lo(u):
                dve.wait_ge(x2hi_done, u + 1)
                dve.tensor_tensor(x2lo[:, bass.ds(u * UT, UT)], bank[7][:], x2hi[:, bass.ds(u * UT, UT)], ALU.subtract).then_inc(x2lo_done, 1)

            ROUTER = 15

            def tail_router(u):
                step = [ROUTER * u]

                def done(ins):
                    ins.then_inc(router, 1)
                    step[0] = step[0] + 1
                    dve.wait_ge(router, step[0])

                dve.wait_ge(lg_ps, u + 1)
                lg = bank[7][:, 0:UB * E].rearrange("p (b e) -> p b e", b=UB)
                dve.tensor_tensor(conf[:], lg, cb_b[:].unsqueeze(1).to_broadcast([P, UB, E]), ALU.add).then_inc(lg_done, 1)
                dve.wait_ge(lg_exp, u + 1)
                done(dve.tensor_scalar(conf[:], conf_e[:], 1.0, None, ALU.add))
                done(dve.reciprocal(conf_e[:], conf[:]))
                done(dve.tensor_tensor(bids[:], conf_e[:], wealth_b[:].unsqueeze(1).to_broadcast([P, UB, E]), ALU.mult))
                dve.memset(carrier[:], 0.0)
                for b in range(UB):
                    dve.max(top[:, b, :], bids[:, b, :]).then_inc(top_done, 1)
                dve.wait_ge(top_done, UB * (u + 1))
                dve.tensor_tensor(vdiff[:], top[:, :, 1], top[:, :, 0], ALU.subtract).then_inc(vdiff_done, 1)
                for b in range(UB):
                    ins = dve.max_index(topi[:, b, :], top[:, b, :], bids[:, b, :])
                    if b < UB - 1:
                        ins.then_inc(router, 1)
                        step[0] = step[0] + 1
                done(ins)
                for s in range(2):
                    ins = dve.tensor_tensor(hot[:, s], iota8[:].unsqueeze(1).to_broadcast([P, UB, E]),
                                            topi[:, :, s:s + 1].to_broadcast([P, UB, E]), ALU.is_equal)
                    ins.then_inc(router, 1)
                    step[0] = step[0] + 1
                dve.wait_ge(vexp_act, u + 1)
                done(dve.tensor_scalar(vdiff[:], vexp[:], 1.0, None, ALU.add))
                done(dve.reciprocal(wts[:, 0, :], vdiff[:]))
                done(dve.tensor_tensor(wts[:, 1, :], wts[:, 0, :], vexp[:], ALU.mult))
                for s in range(2):
                    done(dve.scalar_tensor_tensor(hot[:, s], hot[:, s], 1.0 / WSCALE,
                                                  wts[:, s, :].unsqueeze(2).to_broadcast([P, UB, E]), ALU.mult, ALU.mult))
                dve.tensor_tensor(comb[:, bass.ds(u * UB, UB), :], hot[:, 0], hot[:, 1], ALU.add).then_inc(router, 1)
                assert isinstance(u, int) is False or step[0] + 1 == ROUTER * (u + 1), step[0] + 1 - ROUTER * u

            def weights(u, m):
                dve.wait_ge(whi_done, 3 * u + m + 1)
                cols = bass.ds(u * (3 * I) + m * I, I)
                dve.scalar_tensor_tensor(w_lo[:, cols], bank[2 + m % 2][:], WSCALE, w_hi[:, cols], ALU.mult, ALU.subtract).then_inc(wlo_done, 1)

            def body(u, par):
                if not last(u):
                    wait_x(u + 1, 1 - par)
                if not first(u):
                    tail_o(u - 1, 1 - par)
                mask_scores(u, 0)
                if not last(u):
                    front_stats(u + 1, 1 - par)
                weights(u, 0)
                if not last(u):
                    wait_stats1(u + 1)
                mask_scores(u, 1)
                if not last(u):
                    aggregate(mv1, stats1, mv1_done)
                weights(u, 1)
                if not last(u):
                    front_norm(u + 1, 1 - par)
                mask_scores(u, 2)
                if not first(u):
                    tail_x1(u - 1)
                    wait_x1(u - 1)
                mask_scores(u, 3)
                if not first(u):
                    stats(u - 1, stats2, stats2_done)
                weights(u, 2)
                if not first(u):
                    wait_stats2(u - 1)
                mask_scores(u, 4)
                if not first(u):
                    aggregate(mv2, stats2, mv2_done)
                if not last(u):
                    front_qk(u + 1, 1 - par)
                if not first(u):
                    tail_norm(u - 1)
                mask_scores(u, 5)
                if not last(u):
                    front_v(u + 1, 1 - par)
                mask_scores(u, 6)
                if not first(u):
                    tail_lo(u - 1)
                if not last(u):
                    front_z(u + 1, 1 - par)
                mask_scores(u, 7)
                if not last(u):
                    front_state(u + 1, 1 - par)
                if not first(u):
                    tail_router(u - 1)

            dve.wait_ge(const_loaded, 16 * N_LOADS)
            dve.wait_ge(const_made, N_MADE)
            for b_c, b_n, b_1 in ((bq_c, bq_neg, bq_one), (bk_c, bk_neg, bk_one)):
                dve.tensor_scalar(b_n[:], b_c[:], -1.0, None, ALU.mult).then_inc(const_dve, 1)
                dve.tensor_scalar(b_1[:], b_c[:], 1.0, None, ALU.add).then_inc(const_dve, 1)
            dve.tensor_reduce(headmask[:], headsel[:].rearrange("p r j -> p j r"), AX_X, ALU.add).then_inc(const_dve, 1)
            dve.wait_ge(confT_ps, 1)
            dve.tensor_copy(confT[:], bank[7][:, 0:E]).then_inc(const_dve, 1)
            dve.wait_ge(const_dve, 6)
            wait_x(0, 0)
            front_stats(0, 0)
            wait_stats1(0)
            aggregate(mv1, stats1, mv1_done)
            front_norm(0, 0)
            front_qk(0, 0)
            front_v(0, 0)
            front_z(0, 0)
            front_state(0, 0)
            steady(Units(dve, body))
            tail_o(UNITS - 1, (UNITS - 1) % 2)
            tail_x1(UNITS - 1)
            wait_x1(UNITS - 1)
            stats(UNITS - 1, stats2, stats2_done)
            wait_stats2(UNITS - 1)
            aggregate(mv2, stats2, mv2_done)
            tail_norm(UNITS - 1)
            tail_lo(UNITS - 1)
            tail_router(UNITS - 1)

            with dve.Fori(0, E) as e:
                with dve.Fori(0, UNITS) as g:
                    n = e * UNITS + g
                    for c in range(IC):
                        dve.wait_ge(silu_done, IC * n + c + 1)
                        dve.scalar_tensor_tensor(hid[:, c % 2, :], bank[2 + c % 2][:], 1.0 / WSCALE, silu[:, c % 2, :],
                                                 ALU.mult, ALU.mult).then_inc(hid_done, 1)
                    dve.wait_ge(y_ps, n + 1)
                    for b in range(UB):
                        t = g * UB + b
                        xt = x_all[:, bass.ds(t, 1), :].rearrange("p o d -> p (o d)")
                        w = comb[:].rearrange("p t e -> p (t e)")[:, bass.ds(t * E + e, 1)]
                        dve.scalar_tensor_tensor(xt, bank[4][:, b * P:(b + 1) * P], w, xt, ALU.mult, ALU.add).then_inc(acc_done, 1)

        @block.tensor
        def _(pe):
            def weights(u, par, m):
                if m == 0:
                    pe.wait_ge(w_loaded[par], 48 * (u // 2) + 48)
                    if not first(u):
                        pe.wait_ge(vexp_done, 10 * (u + 1))
                elif m == 2:
                    pe.wait_ge(wlo_done, 3 * u + 1)
                for c in range(IC):
                    ins = pe.transpose(bank[2 + m % 2][:, c * P:(c + 1) * P], w_raw[par][:, m, c * P:(c + 1) * P], ident[:])
                ins.then_inc(w_ps, 1)

            def front_transposes(u, par):
                pe.wait_ge(xhat_done, UB * (u + 1))
                if not first(u):
                    pe.wait_ge(ktok_copied, u)
                for b in range(UB):
                    ins = pe.transpose(bank[0][:, b * L:(b + 1) * L], xhat[:, b, :], ident[:])
                ins.then_inc(xT_ps, 1)
                pe.wait_ge(ctx_loaded[par], 16 * (u // 2) + 16)
                if not first(u):
                    pe.wait_ge(state_done, u)
                for b in range(UB):
                    ins = pe.transpose(bank[1][:, b * L:(b + 1) * L], ctx_s[par][:, b, :], ident[:])
                ins.then_inc(cT_ps, 1)

            def front_project(u, par):
                pe.wait_ge(xT_copied, u + 1)
                pe.matmul(bank[0][:], Wq_s[:], xT[:], start=True, stop=True).then_inc(q_ps, 1)
                pe.wait_ge(cT_copied, u + 1)
                pe.matmul(bank[1][:], Wk_s[:], cT[:, :, 0, :], start=True, stop=True).then_inc(k_ps, 1)
                if isinstance(u, int) and u == 0:
                    pass
                else:
                    pe.wait_ge(wlo_done, 3 * u)
                for c in range(NCH):
                    ins = pe.matmul(bank[2 + c // 4][:, (c % 4) * P:(c % 4 + 1) * P], cT[:, c, :, :], Wv_s[:], start=True, stop=True)
                ins.then_inc(v_ps, 1)

            def front_ktok(u, par):
                pe.wait_ge(qk_done, 2 * u + 2)
                for b in range(UB):
                    ins = pe.transpose(bank[0][:, b * P:(b + 1) * P], kT[:, b * L:(b + 1) * L], ident[:])
                ins.then_inc(ktok_ps, 1)

            def front_state(u, par):
                pe.wait_ge(ktok_copied, u + 1)
                pe.wait_ge(vexp_done, 10 * (u + 1))
                for b in range(UB):
                    ins = pe.matmul(bank[1][:, b * P:(b + 1) * P], Ktok[:, b, :], Vtok[:, b, :], start=True, stop=True)
                ins.then_inc(state_ps, 1)

            def scores(u, par, t):
                bb, r = t // RG, t % RG
                rows = slice(32 * r, 32 * r + 32)
                if t == 0:
                    pe.wait_ge(kexp_done, 4 * (u + 1))
                if t >= 2:
                    pe.wait_ge(p_done, NBLK * u + t - 1)
                elif not first(u):
                    pe.wait_ge(p_done, NBLK * u + t - 1)
                for n in range(4):
                    c = bb * 4 + n
                    for j in range(2):
                        ins = pe.matmul(bank[4 + t % 2][:, (n * 2 + j) * CH:(n * 2 + j + 1) * CH],
                                        Kexp[par][rows, c, 2 * j:2 * j + 2, :], qT[par][rows, c * CH:(c + 1) * CH],
                                        start=True, stop=True)
                ins.then_inc(scores_ps, 1)

            def values(u, par, t):
                bb, r = t // RG, t % RG
                rows = slice(32 * r, 32 * r + 32)
                if t == 0:
                    pe.wait_ge(state_done, u + 1)
                    if not first(u):
                        pe.wait_ge(o_done, u)
                    for b in range(UB):
                        pe.matmul(bank[6][:, b * L + CH:(b + 1) * L], state[par][:, b, :], qT[par][:, b * L + CH:(b + 1) * L],
                                  start=(b == 0), stop=False, skip_group_check=True)
                pe.wait_ge(p_done, NBLK * u + t + 1)
                for n in range(4):
                    c = bb * 4 + n
                    for j in range(2):
                        ins = pe.matmul(bank[6][rows, c * CH:(c + 1) * CH], Vexp[par][:, c, r, j, :],
                                        Pm[:, t % 4, (n * 2 + j) * CH:(n * 2 + j + 1) * CH],
                                        start=False, stop=(j == 1), skip_group_check=True)
                ins.then_inc(av_done, 1)

            def tail_out(u):
                pe.wait_ge(o_done, u + 1)
                if not first(u):
                    pe.wait_ge(lg_done, u)
                for b in range(UB):
                    ins = pe.matmul(bank[7][:, b * P:(b + 1) * P], oT[:, b * L:(b + 1) * L], Wo_s[:], start=True, stop=True)
                ins.then_inc(ao_ps, 1)

            def tail_x2(u):
                pe.wait_ge(x2hat_done, UB * (u + 1))
                for b in range(UB):
                    ins = pe.transpose(bank[7][:, b * L:(b + 1) * L], x2hat[:, b, :], ident[:])
                ins.then_inc(x2T_ps, 1)

            def tail_logits(u):
                pe.wait_ge(x2T_copied, u + 1)
                pe.wait_ge(x2lo_done, u + 1)
                for b in range(UB):
                    ins = pe.matmul(bank[7][:, b * E:(b + 1) * E], x2T[:, b * L:(b + 1) * L], confT[:], start=True, stop=True)
                ins.then_inc(lg_ps, 1)

            def body(u, par):
                scores(u, par, 0)
                weights(u, par, 0)
                scores(u, par, 1)
                if not first(u):
                    tail_out(u - 1)
                weights(u, par, 1)
                values(u, par, 0)
                scores(u, par, 2)
                values(u, par, 1)
                scores(u, par, 3)
                if not last(u):
                    front_transposes(u + 1, 1 - par)
                weights(u, par, 2)
                values(u, par, 2)
                scores(u, par, 4)
                if not last(u):
                    front_project(u + 1, 1 - par)
                values(u, par, 3)
                scores(u, par, 5)
                values(u, par, 4)
                scores(u, par, 6)
                if not first(u):
                    tail_x2(u - 1)
                if not last(u):
                    front_ktok(u + 1, 1 - par)
                values(u, par, 5)
                scores(u, par, 7)
                values(u, par, 6)
                if not last(u):
                    front_state(u + 1, 1 - par)
                if not first(u):
                    tail_logits(u - 1)
                values(u, par, 7)

            pe.wait_ge(const_made, N_MADE)
            pe.wait_ge(const_loaded, 16 * N_LOADS)
            pe.transpose(bank[7][:, 0:E], conf_s[:], ident[0:E, 0:E]).then_inc(confT_ps, 1)
            front_transposes(0, 0)
            front_project(0, 0)
            front_ktok(0, 0)
            front_state(0, 0)
            steady(Units(pe, body))
            tail_out(UNITS - 1)
            tail_x2(UNITS - 1)
            tail_logits(UNITS - 1)

            pe.wait_ge(wlo_done, 3 * E)
            pe.wait_ge(router, 15 * UNITS)
            with pe.Fori(0, E) as e:
                with pe.Fori(0, UNITS) as g:
                    n = e * UNITS + g

                    def gate_up(c):
                        if c >= 2:
                            pe.wait_ge(hid_done, IC * n + c - 1)
                        for m in range(2):
                            ps = bank[2 * m + c % 2]
                            col = e * (3 * I) + (m * I + c * P)
                            tok = bass.ds(g * UT, UT)
                            pe.matmul(ps[:], w_hi[:, bass.ds(col, P)], x2hi[:, tok], start=True, stop=False)
                            pe.matmul(ps[:], w_hi[:, bass.ds(col, P)], x2lo[:, tok], start=False, stop=False)
                            ins = pe.matmul(ps[:], w_lo[:, bass.ds(col, P)], x2hi[:, tok], start=False, stop=True)
                        ins.then_inc(gu_ps, 1)

                    def down(c):
                        pe.wait_ge(lo_done, IC * n + c + 1)
                        col = e * (3 * I) + (2 * I + c * P)
                        for b in range(UB):
                            ps = bank[4][:, b * P:(b + 1) * P]
                            tok = slice(b * P, (b + 1) * P)
                            pe.matmul(ps, hid_hi[:, c % 2, tok], w_hi[:, bass.ds(col, P)], start=(c == 0 and b == 0), stop=False, skip_group_check=True)
                            pe.matmul(ps, hid_hi[:, c % 2, tok], w_lo[:, bass.ds(col, P)], start=False, stop=False, skip_group_check=True)
                            ins = pe.matmul(ps, hid_lo[:, c % 2, tok], w_hi[:, bass.ds(col, P)], start=False, stop=(c == IC - 1), skip_group_check=True)
                        if c == IC - 1:
                            ins.then_inc(y_ps, 1)
                        else:
                            ins.then_inc(hid_used, 1)

                    gate_up(0)
                    gate_up(1)
                    down(0)
                    gate_up(2)
                    down(1)
                    gate_up(3)
                    down(2)
                    down(3)


_INS = ['x', 'ctx_1024', 'L0_xattn_Wq', 'L0_xattn_bq', 'L0_xattn_Wk', 'L0_xattn_bk', 'L0_xattn_Wv', 'L0_xattn_bv',
        'L0_xattn_Wo', 'L0_xattn_bo', 'L0_ffn_conf_w', 'L0_ffn_conf_b', 'L0_ffn_gate_w', 'L0_ffn_up_w',
        'L0_ffn_down_w', 'L0_ffn_wealth']


def kernel(**inputs):
    import numpy as _np
    import concourse.bacc as _bacc
    from concourse import mybir as _mybir
    from concourse.bass_utils import run_bass_kernel_spmd as _run

    nc = _bacc.Bacc("TRN2", target_bir_lowering=False, num_devices=1)
    arrays, args = {}, []
    for name in _INS:
        a = _np.ascontiguousarray(inputs[name])
        arrays[f"in_{name}_dram"] = a
        args.append(nc.dram_tensor(f"in_{name}_dram", a.shape, _mybir.dt.from_np(a.dtype), kind="ExternalInput").ap())
    shape = arrays["in_x_dram"].shape
    args.append(nc.dram_tensor("out_dram", shape, _mybir.dt.float32, kind="ExternalOutput").ap())
    attention_moe_kernel(nc, *args)
    r = _run(nc, [arrays], core_ids=[0])
    return r.results[0]["out_dram"]
```

```python
from contextlib import ExitStack

import concourse.bass as bass
from concourse import mybir

ALU = mybir.AluOpType
ACT = mybir.ActivationFunctionType
AX_X = mybir.AxisListType.X
F32 = mybir.dt.float32
F16 = mybir.dt.float16
BF16 = mybir.dt.bfloat16
U32 = mybir.dt.uint32
I32 = mybir.dt.int32

P = 128
WSCALE = 64.0
EPS = 1e-5


def attention_moe_kernel(nc, x, ctx_in, Wq, bq, Wk, bk, Wv, bv, Wo, bo,
                         conf_w, conf_b, gate_w, up_w, down_w, wealth, out):
    NB, L, D = x.shape
    E, I, _ = gate_w.shape
    H, HD = 16, D // 16
    UB = 4
    UNITS = NB // UB
    UT = UB * L
    CH = 64
    NCH = UB * L // CH
    RG = 4
    NBLK = 2 * RG
    IC = I // P
    TOP = 2
    NT = NB * L
    REGION = NT + P
    ROW = D + 2
    TILES = NT * TOP // P + E
    FAR = 4.0 * NT
    assert L == P and D == P and E == UNITS and HD == 8 and L == 2 * CH

    with ExitStack() as ctx:
        def sb(name, shape, dt=F32):
            return ctx.enter_context(nc.sbuf_tensor(name, shape, dt))

        def sem(name):
            return ctx.enter_context(nc.semaphore(name))

        ident = sb("ident", [P, P])
        causal = sb("causal", [P, CH])
        headmask = sb("headmask", [P, 4])
        headsel = sb("headsel", [P, RG, 4])
        blockdiag = sb("blockdiag", [P, P])
        ones = sb("ones", [P, P])
        minus_half = sb("minus_half", [P, UB])
        eps = sb("eps", [P, UB])
        carrier = sb("carrier", [P, 1])
        iota8 = sb("iota8", [P, E])
        Wq_s, Wk_s, Wv_s, Wo_s = (sb(n, [P, P]) for n in ("Wq_s", "Wk_s", "Wv_s", "Wo_s"))
        bq_c, bk_c = sb("bq_c", [P, 1]), sb("bk_c", [P, 1])
        bq_neg, bk_neg = sb("bq_neg", [P, 1]), sb("bk_neg", [P, 1])
        bq_one, bk_one = sb("bq_one", [P, 1]), sb("bk_one", [P, 1])
        bv_b, bo_b = sb("bv_b", [P, P]), sb("bo_b", [P, P])
        cb_b, wealth_b = sb("cb_b", [P, E]), sb("wealth_b", [P, E])
        conf_s = sb("conf_s", [E, P])
        confT = sb("confT", [P, E])
        x_all = sb("x_all", [P, NB, P])
        ctx_s = [sb(f"ctx_s{i}", [P, UB, P]) for i in range(2)]
        stats1 = sb("stats1", [P, UB, 6])
        mv1 = sb("mv1", [P, UB, 2])
        ve1 = sb("ve1", [P, UB])
        rstd1 = sb("rstd1", [P, UB])
        xhat = sb("xhat", [P, UB, P])
        xT = sb("xT", [P, UT])
        cT = sb("cT", [P, NCH, 2, CH])
        neg = sb("neg", [P, 2, UT])
        expn = sb("expn", [P, 2, UT])
        qT = [sb(f"qT{i}", [P, UT]) for i in range(2)]
        kT = sb("kT", [P, UT])
        Kexp = [sb(f"Kexp{i}", [P, NCH, 4, CH]) for i in range(2)]
        Vexp = [sb(f"Vexp{i}", [P, NCH, RG, 2, 32]) for i in range(2)]
        Vtok = sb("Vtok", [CH, UB, P])
        Ktok = sb("Ktok", [CH, UB, P])
        state = [sb(f"state{i}", [P, UB, P]) for i in range(2)]
        Z = sb("Z", [P, UT])
        rZ = [sb(f"rZ{i}", [P, UT]) for i in range(2)]
        Pm = sb("Pm", [P, 4, UT])
        oT = sb("oT", [P, UT])
        stats2 = sb("stats2", [P, UB, 6])
        mv2 = sb("mv2", [P, UB, 2])
        ve2 = sb("ve2", [P, UB])
        rstd2 = sb("rstd2", [P, UB])
        x2hat = [sb(f"x2hat{i}", [P, UB, P]) for i in range(2)]
        x2T = sb("x2T", [P, UT])
        conf = sb("conf", [P, UB, E])
        conf_e = sb("conf_e", [P, UB, E])
        bids = sb("bids", [P, UB, E])
        top = sb("top", [P, UB, 8])
        topi = sb("topi", [P, UB, 8], U32)
        vdiff = sb("vdiff", [P, UB])
        vexp = sb("vexp", [P, UB])
        wts = sb("wts", [P, UB])
        hot = sb("hot", [P, TOP, UB, E])
        chosen = sb("chosen", [P, UB, E], BF16)
        chosen_sum = sb("chosen_sum", [P, E])
        before = sb("before", [P, E], BF16)
        earlier = sb("earlier", [P, P], BF16)
        ones_b = sb("ones_b", [P, P], BF16)
        region = sb("region", [P, E])
        rank = sb("rank", [P, UB, E])
        place = sb("place", [P, TOP, UB, E])
        rows_to = sb("rows_to", [P, TOP, UB], U32)
        pair_id = sb("pair_id", [P, UB, TOP])
        unit_ids = sb("unit_ids", [P, UB, TOP])
        unit_start = sb("unit_start", [P, UB, TOP])
        token_rows = sb("token_rows", [P, UB, TOP, ROW])
        row_halves = token_rows[:].rearrange("p b s r -> p (b s r)").bitcast(F16).rearrange("p (b s r) -> p b s r", b=UB, s=TOP)
        pad_row = sb("pad_row", [P, ROW])
        ident_h = sb("ident_h", [P, P], F16)
        tile_no = sb("tile_no", [1, TILES])
        count = sb("count", [1, E])
        pad_at = sb("pad_at", [1, E], I32)
        blocks_u = sb("blocks_u", [1, E], U32)
        blocks_s = sb("blocks_s", [1, E], U32)
        blocks = sb("blocks", [1, E])
        blocks_to = sb("blocks_to", [1, E])
        passed = sb("passed", [1, TILES, E])
        passed_blocks = sb("passed_blocks", [1, TILES, E])
        tile_expert = sb("tile_expert", [1, TILES])
        tile_start = sb("tile_start", [1, TILES])
        tile_row = sb("tile_row", [1, TILES])
        row_at = sb("row_at", [1, TILES], I32)
        col_at = sb("col_at", [1, TILES], I32)
        w_raw = [sb(f"w_raw{i}", [P, 3, IC * P]) for i in range(2)]
        w_hi = sb("w_hi", [P, E * 3 * IC * P], F16)
        w_lo = sb("w_lo", [P, E * 3 * IC * P], F16)
        xg = sb("xg", [P, 4, ROW])
        xg_halves = xg[:].rearrange("p k r -> p (k r)").bitcast(F16).rearrange("p (k r) -> p k r", k=4)
        xgT = sb("xgT", [P, 2, 2 * P], F16)
        y_to = sb("y_to", [P, 4], U32)
        y_scale = sb("y_scale", [P, 4])
        silu = sb("silu", [P, 2, UT])
        silu_warm = sb("silu_warm", [P, 1])
        hid = sb("hid", [P, 2, UT])
        hid_hi = sb("hid_hi", [P, 2, UT], F16)
        hid_lo = sb("hid_lo", [P, 2, UT], F16)
        y_sb = sb("y_sb", [P, 4, P])
        BACK = UNITS // 2 * UB * TOP * P
        y_back = [w[:, 0:2 * BACK].bitcast(F32).rearrange("p (u b s d) -> p u b s d", u=UNITS // 2, b=UB, s=TOP)
                  for w in (w_hi, w_lo)]

        by_expert = nc.dram_tensor("by_expert", (E * REGION + P, ROW), F32, kind="Internal").ap()
        by_token = nc.dram_tensor("by_token", (NT * TOP, D), F32, kind="Internal").ap()

        bank = [ctx.enter_context(nc.psum_tensor(f"bank{i}", [P, 512], F32)) for i in range(8)]

        const_loaded = sem("const_loaded")
        const_made = sem("const_made")
        const_dve = sem("const_dve")
        confT_ps = sem("confT_ps")
        x_loaded = [sem(f"x_loaded{i}") for i in range(2)]
        ctx_loaded = [sem(f"ctx_loaded{i}") for i in range(2)]
        w_loaded = [sem(f"w_loaded{i}") for i in range(2)]
        stats1_done = sem("stats1_done")
        mv1_done = sem("mv1_done")
        ve1_done = sem("ve1_done")
        rstd1_done = sem("rstd1_done")
        xhat_done = sem("xhat_done")
        xb_done = sem("xb_done")
        xT_ps = sem("xT_ps")
        cT_ps = sem("cT_ps")
        xT_copied = sem("xT_copied")
        cT_copied = sem("cT_copied")
        q_ps = sem("q_ps")
        k_ps = sem("k_ps")
        v_ps = sem("v_ps")
        neg_done = sem("neg_done")
        exp_done = sem("exp_done")
        qk_done = sem("qk_done")
        kexp_done = sem("kexp_done")
        vexp_done = sem("vexp_done")
        ktok_ps = sem("ktok_ps")
        ktok_copied = sem("ktok_copied")
        state_ps = sem("state_ps")
        state_done = sem("state_done")
        z_done = sem("z_done")
        rz_done = sem("rz_done")
        scores_ps = sem("scores_ps")
        p_done = sem("p_done")
        av_done = sem("av_done")
        o_done = sem("o_done")
        ao_ps = sem("ao_ps")
        x1_done = sem("x1_done")
        stats2_done = sem("stats2_done")
        mv2_done = sem("mv2_done")
        ve2_done = sem("ve2_done")
        rstd2_done = sem("rstd2_done")
        x2hat_done = sem("x2hat_done")
        x2T_ps = sem("x2T_ps")
        x2T_copied = sem("x2T_copied")
        row_hi_done = sem("row_hi_done")
        row_lo_done = sem("row_lo_done")
        row_id_done = sem("row_id_done")
        id_next = sem("id_next")
        lg_ps = sem("lg_ps")
        lg_done = sem("lg_done")
        lg_exp = sem("lg_exp")
        router = sem("router")
        top_done = sem("top_done")
        vdiff_done = sem("vdiff_done")
        vexp_act = sem("vexp_act")
        weights_done = sem("weights_done")
        rank_ps = sem("rank_ps")
        placing = sem("placing")
        before_done = sem("before_done")
        rows_to_done = sem("rows_to_done")
        dispatched = sem("dispatched")
        padded = sem("padded")
        count_ps = sem("count_ps")
        pad_at_done = sem("pad_at_done")
        table = sem("table")
        w_ps = sem("w_ps")
        whi_done = sem("whi_done")
        wlo_done = sem("wlo_done")
        xg_loaded = [sem(f"xg_loaded{i}") for i in range(4)]
        xgT_ps = sem("xgT_ps")
        xgT_copied = sem("xgT_copied")
        y_to_done = sem("y_to_done")
        gate_ps = sem("gate_ps")
        up_ps = sem("up_ps")
        silu_done = sem("silu_done")
        hid_done = sem("hid_done")
        hi_done = sem("hi_done")
        lo_done = sem("lo_done")
        y_ps = sem("y_ps")
        y_done = sem("y_done")
        y_stored = [sem(f"y_stored{i}") for i in range(4)]
        y_loaded = [sem(f"y_loaded{i}") for i in range(UNITS)]
        sum_done = sem("sum_done")
        out_done = sem("out_done")
        stored = sem("stored")

        block = ctx.enter_context(nc.Block())

        x_tok = x.rearrange("b t d -> t b d")
        ctx_tok = ctx_in.rearrange("b t d -> t b d")
        out_tok = out.rearrange("b t d -> t b d")
        N_LOADS = 11
        TABLE = 15
        N_MADE = 24

        def steady(run):
            run(0, 0)
            with run.engine.Fori(0, (UNITS - 2) // 2) as i:
                run(i * 2 + 1, 1)
                run(i * 2 + 2, 0)
            run(UNITS - 1, (UNITS - 1) % 2)

        class Units:

            def __init__(self, engine, body):
                self.engine, self.body = engine, body

            def __call__(self, u, par):
                self.body(u, par)

        def tiles(engine, step, ahead=0):
            for i in range(4):
                step(i, i)
            with engine.Fori(0, TILES // 4 - 2) as n:
                for k in range(4):
                    step(n * 4 + (4 + k), k)
            for i in range(TILES - 4, TILES + ahead):
                step(i, i % 4)

        def at_least(i, n):
            return not isinstance(i, int) or i >= n

        def before_end(i, n=TILES):
            return not isinstance(i, int) or i < n

        def first(u):
            return isinstance(u, int) and u == 0

        def last(u):
            return isinstance(u, int) and u == UNITS - 1

        @block.sync
        def _(sp):
            def load_unit(u, par):
                if not (isinstance(u, int) and u < 2):
                    sp.wait_ge(x_loaded[par], 16 * ((u - par) // 2) if isinstance(u, int) else 16 * (u // 2))
                sp.dma_start(x_all[:, bass.ds(u * UB, UB), :], x_tok[:, bass.ds(u * UB, UB), :]).then_inc(x_loaded[par], 16)
                if not (isinstance(u, int) and u < 2):
                    sp.wait_ge(cT_ps, u - 1)
                sp.dma_start(ctx_s[par][:], ctx_tok[:, bass.ds(u * UB, UB), :]).then_inc(ctx_loaded[par], 16)

            def load_w(u, par):
                if not (isinstance(u, int) and u < 2):
                    sp.wait_ge(w_ps, 3 * (u - 1))
                for m, w in enumerate((gate_w, up_w)):
                    sp.dma_start(w_raw[par][:, m, :].rearrange("p (c h) -> p c h", c=IC),
                                 w[bass.ds(u, 1), :, :].rearrange("o (c p) h -> p (o c) h", p=P)).then_inc(w_loaded[par], 16)
                sp.dma_start(w_raw[par][:, 2, :],
                             down_w[bass.ds(u, 1), :, :].rearrange("o h i -> h (o i)")).then_inc(w_loaded[par], 16)

            load_unit(0, 0)
            for dst, src in ((Wq_s, Wq), (Wk_s, Wk), (Wv_s, Wv), (Wo_s, Wo), (conf_s, conf_w)):
                sp.dma_start(dst[:], src).then_inc(const_loaded, 16)
            for dst, src in ((bv_b, bv), (bo_b, bo), (cb_b, conf_b), (wealth_b, wealth)):
                sp.dma_start(dst[:], src.partition_broadcast(P)).then_inc(const_loaded, 16)
            for dst, src in ((bq_c, bq), (bk_c, bk)):
                sp.dma_start(dst[:], src.unsqueeze(1)).then_inc(const_loaded, 16)
            load_w(0, 0)
            load_unit(1, 1)
            load_w(1, 1)
            with sp.Fori(0, (UNITS - 2) // 2) as i:
                for par in range(2):
                    load_unit(i * 2 + 2 + par, par)
                    load_w(i * 2 + 2 + par, par)
            sp.wait_ge(const_made, N_MADE)
            sp.dma_start(by_expert[E * REGION:E * REGION + P, :], pad_row[:]).then_inc(padded, 16)
            sp.wait_ge(pad_at_done, 1)
            for e in range(E):
                at = sp.value_load(pad_at[0:1, e:e + 1], min_val=e * REGION, max_val=e * REGION + NT)
                sp.dma_start(by_expert[bass.ds(at, P), :], pad_row[:]).then_inc(padded, 16)
            sp.wait_ge(padded, 16 * (E + 1))
            sp.wait_ge(table, TABLE)

            def load_tile(i, k):
                at = sp.value_load(row_at[0:1, bass.ds(i, 1)], min_val=0, max_val=E * REGION)
                if at_least(i, 4):
                    sp.wait_ge(y_to_done, 2 * (i - 3))
                    sp.wait_ge(xgT_ps, i - 3)
                sp.wait_ge(dispatched, 16 * NB * TOP)
                sp.dma_start(xg[:, k, :], by_expert[bass.ds(at, P), :]).then_inc(xg_loaded[k], 16)

            tiles(sp, load_tile)

            for k in range(4):
                sp.wait_ge(y_stored[k], 16 * (TILES // 4))
            back = by_token.rearrange("(u b t s) d -> u t b s d", u=UNITS, b=UB, s=TOP)
            for u in range(UNITS):
                sp.dma_start(y_back[u % 2][:, u // 2], back[u]).then_inc(y_loaded[u], 16)
            for u in range(UNITS):
                sp.wait_ge(out_done, u + 1)
                sp.dma_start(out_tok[:, bass.ds(u * UB, UB), :], x_all[:, bass.ds(u * UB, UB), :]).then_inc(stored, 16)
            sp.wait_ge(stored, 16 * UNITS)


        @block.gpsimd
        def _(pool):
            n_made = [0]

            def made(ins):
                ins.then_inc(const_made, 1)
                n_made[0] += 1
                pool.wait_ge(const_made, n_made[0])

            made(pool.memset(ones[:], 1.0))
            made(pool.memset(minus_half[:], -0.5))
            made(pool.memset(eps[:], EPS))
            for i in range(2):
                made(pool.memset(Vexp[i][:], 0.0))
            made(pool.affine_select(ident[:], ones[:], [[1, P]], ALU.is_equal, 0.0, base=0, channel_multiplier=-1))
            for half in range(2):
                rows = slice(half * CH, half * CH + CH)
                made(pool.affine_select(causal[rows, :], ones[rows, 0:CH], [[1, CH]], ALU.is_ge, 0.0, base=0, channel_multiplier=-1))
            ones_h = ones[:, 0:H].rearrange("p (r j) -> p r j", r=RG)
            made(pool.affine_select(headsel[:], ones_h, [[-4 * HD, RG], [-HD, 4]], ALU.is_ge, 0.0, base=0, channel_multiplier=1))
            made(pool.affine_select(headsel[:], headsel[:], [[4 * HD, RG], [HD, 4]], ALU.is_ge, 0.0, base=HD - 1, channel_multiplier=-1))
            bd = blockdiag[:].rearrange("p (h k) -> p h k", h=H)
            made(pool.affine_select(bd, ones[:].rearrange("p (h k) -> p h k", h=H), [[-HD, H], [0, HD]], ALU.is_ge, 0.0, base=0, channel_multiplier=1))
            made(pool.affine_select(bd, bd, [[HD, H], [0, HD]], ALU.is_ge, 0.0, base=HD - 1, channel_multiplier=-1))
            made(pool.iota(iota8[:], [[1, E]], base=0, channel_multiplier=0, allow_small_or_imprecise_dtypes=True))
            made(pool.tensor_copy(ident_h[:], ident[:]))
            made(pool.memset(ones_b[:], 1.0))
            made(pool.affine_select(earlier[:], ones_b[:], [[1, P]], ALU.is_gt, 0.0, base=0, channel_multiplier=-1))
            made(pool.iota(region[:], [[REGION, E]], base=0, channel_multiplier=0, allow_small_or_imprecise_dtypes=True))
            made(pool.iota(pair_id[:], [[TOP * L, UB], [1, TOP]], base=0, channel_multiplier=TOP, allow_small_or_imprecise_dtypes=True))
            made(pool.iota(tile_no[:], [[1, TILES]], base=0, channel_multiplier=0, allow_small_or_imprecise_dtypes=True))
            made(pool.memset(before[:], 0.0))
            made(pool.memset(unit_ids[:], float(TOP * UT)))
            made(pool.memset(unit_start[:], 0.0))
            made(pool.memset(pad_row[:], 0.0))
            made(pool.memset(pad_row[:, D + 1:D + 2], FAR))
            pool.wait_ge(const_loaded, 16 * N_LOADS)
            pool.wait_ge(const_made, N_MADE)

            def rstd(mv_done, mv, ve, ve_done, rs, rs_done, u):
                pool.wait_ge(mv_done, UB * (u + 1))
                pool.tensor_tensor(ve[:], mv[:, :, 1], eps[:], ALU.add).then_inc(ve_done, 1)
                pool.wait_ge(ve_done, u + 1)
                pool.tensor_tensor(rs[:], ve[:], minus_half[:], ALU.pow).then_inc(rs_done, 1)

            def front(u):
                rstd(mv1_done, mv1, ve1, ve1_done, rstd1, rstd1_done, u)
                pool.wait_ge(xhat_done, UB * (u + 1))
                xu = x_all[:, bass.ds(u * UB, UB), :]
                pool.tensor_tensor(xu, xu, bo_b[:].unsqueeze(1).to_broadcast([P, UB, P]), ALU.add).then_inc(xb_done, 1)

            def tail(u, par):
                rstd(mv2_done, mv2, ve2, ve2_done, rstd2, rstd2_done, u)
                pool.wait_ge(row_hi_done, u + 1)
                for s in range(TOP):
                    pool.tensor_tensor(row_halves[:, :, s, D:2 * D], x2hat[par][:], row_halves[:, :, s, 0:D], ALU.subtract).then_inc(row_lo_done, 1)
                if not first(u):
                    pool.wait_ge(id_next, u)
                pool.tensor_tensor(token_rows[:, :, :, D + 1], pair_id[:], unit_start[:], ALU.add).then_inc(row_id_done, 1)

            def dispatch(u):
                pool.wait_ge(row_lo_done, TOP * (u + 1))
                pool.wait_ge(weights_done, TOP * (u + 1))
                pool.wait_ge(rows_to_done, u + 1)
                pool.wait_ge(row_id_done, u + 1)
                pool.tensor_tensor(unit_start[:], unit_start[:], unit_ids[:], ALU.add).then_inc(id_next, 1)
                for b in range(UB):
                    for s in range(TOP):
                        pool.indirect_dma_start(by_expert, bass.IndirectOffsetOnAxis(ap=rows_to[:, s, b:b + 1], axis=0),
                                                token_rows[:, b, s, :], None).then_inc(dispatched, 16)

            def body(u, par):
                if not last(u):
                    front(u + 1)
                if not first(u):
                    tail(u - 1, 1 - par)
                    dispatch(u - 1)

            front(0)
            steady(Units(pool, body))
            tail(UNITS - 1, (UNITS - 1) % 2)
            dispatch(UNITS - 1)

            def tile_step(i, k):
                if at_least(i, 2):
                    pool.wait_ge(y_done, i - 1)
                if before_end(i):
                    pool.wait_ge(xg_loaded[k], 16 * (i // 4) + 16)
                    if at_least(i, 4):
                        pool.wait_ge(y_stored[k], 16 * (i // 4))
                    pool.tensor_tensor(y_scale[:, k:k + 1], xg[:, k, D:D + 1], ones[:, 0:1], ALU.mult).then_inc(y_to_done, 1)
                    pool.tensor_copy(y_to[:, k:k + 1], xg[:, k, D + 1:D + 2]).then_inc(y_to_done, 1)
                if at_least(i, 2):
                    kk = (k - 2) % 4
                    pool.indirect_dma_start(by_token, bass.IndirectOffsetOnAxis(ap=y_to[:, kk:kk + 1], axis=0),
                                            y_sb[:, kk, :], None, bounds_check=NT * TOP - 1, oob_is_err=False).then_inc(y_stored[kk], 16)

            tiles(pool, tile_step, 2)

        @block.scalar
        def _(act):
            def weights(u, m):
                act.wait_ge(w_ps, 3 * u + m + 1)
                act.activation(w_hi[:, bass.ds(u * (3 * I) + m * I, I)], bank[2 + m % 2][:], ACT.Copy, scale=WSCALE).then_inc(whi_done, 1)

            def front_copies(u, par):
                act.wait_ge(xT_ps, u + 1)
                act.activation(xT[:], bank[0][:], ACT.Copy).then_inc(xT_copied, 1)
                act.wait_ge(cT_ps, u + 1)
                if not first(u):
                    act.wait_ge(v_ps, u)
                act.activation(cT[:], bank[1][:].rearrange("p (c s) -> p c s", s=CH).unsqueeze(2).to_broadcast([P, NCH, 2, CH]),
                               ACT.Copy).then_inc(cT_copied, 1)

            def front_exp(u, par):
                for m, (ps, ready, bneg) in enumerate(((bank[0], q_ps, bq_neg), (bank[1], k_ps, bk_neg))):
                    act.wait_ge(ready, u + 1)
                    act.activation(neg[:, m, :], ps[:], ACT.Relu, bias=bneg[:], scale=-1.0).then_inc(neg_done, 1)
                    act.wait_ge(neg_done, 2 * u + m + 1)
                    act.activation(expn[:, m, :], neg[:, m, :], ACT.Exp, scale=-1.0).then_inc(exp_done, 1)

            def front_ktok(u, par):
                act.wait_ge(ktok_ps, u + 1)
                act.activation(Ktok[:].rearrange("p b d -> p (b d)"), bank[0][0:CH, :], ACT.Copy).then_inc(ktok_copied, 1)

            def tail_x2(u, par):
                act.wait_ge(x2T_ps, u + 1)
                act.activation(x2T[:], bank[7][:], ACT.Copy).then_inc(x2T_copied, 1)
                if not first(u):
                    act.wait_ge(dispatched, 16 * UB * TOP * u)
                act.activation(row_halves[:, :, :, 0:D], x2hat[par][:].unsqueeze(2).to_broadcast([P, UB, TOP, D]), ACT.Copy).then_inc(row_hi_done, 1)

            def tail_exp1(u):
                act.wait_ge(lg_done, u + 1)
                act.activation(conf_e[:], conf[:], ACT.Exp, scale=-1.0).then_inc(lg_exp, 1)

            def tail_exp2(u):
                act.wait_ge(vdiff_done, u + 1)
                act.activation(vexp[:], vdiff[:], ACT.Exp).then_inc(vexp_act, 1)

            def body(u, par):
                weights(u, 0)
                weights(u, 1)
                if not last(u):
                    front_copies(u + 1, 1 - par)
                weights(u, 2)
                if not first(u):
                    tail_x2(u - 1, 1 - par)
                if not last(u):
                    front_exp(u + 1, 1 - par)
                if not first(u):
                    tail_exp1(u - 1)
                if not last(u):
                    front_ktok(u + 1, 1 - par)
                if not first(u):
                    tail_exp2(u - 1)

            act.wait_ge(const_dve, 6)
            front_copies(0, 0)
            front_exp(0, 0)
            front_ktok(0, 0)
            steady(Units(act, body))
            tail_x2(UNITS - 1, (UNITS - 1) % 2)
            tail_exp1(UNITS - 1)
            tail_exp2(UNITS - 1)

            def tile_step(i, k):
                if before_end(i):
                    act.wait_ge(gate_ps, i + 1)
                    if at_least(i, 2):
                        act.wait_ge(hid_done, i - 1)
                    act.activation(silu[:, k % 2, :], bank[k % 2][:], ACT.Silu, scale=1.0 / WSCALE).then_inc(silu_done, 1)
                if at_least(i, 2):
                    kk = (k - 2) % 4
                    act.wait_ge(y_ps, i - 1)
                    act.wait_ge(y_to_done, 2 * (i - 1))
                    if at_least(i, 6):
                        act.wait_ge(y_stored[kk], 16 * ((i - 2) // 4))
                    act.activation(y_sb[:, kk, :], bank[6 + k % 2][:, 0:P], ACT.Copy, scale=y_scale[:, kk:kk + 1]).then_inc(y_done, 1)
                if before_end(i):
                    act.wait_ge(hid_done, i + 1)
                    act.activation(hid_hi[:, k % 2, :], hid[:, k % 2, :], ACT.Copy).then_inc(hi_done, 1)

            act.activation(silu_warm[:], bq_one[:], ACT.Silu)
            tiles(act, tile_step, 2)

        @block.vector
        def _(dve):
            def stats(u, st, st_done):
                for b in range(UB):
                    dve.bn_stats(st[:, b, :], x_all[:, bass.ds(u * UB + b, 1), :].rearrange("p o d -> p (o d)")).then_inc(st_done, 1)

            def aggregate(mv, st, mv_done):
                for b in range(UB):
                    dve.bn_aggr(mv[:, b, :], st[:, b, :]).then_inc(mv_done, 1)

            def wait_x(u, par):
                dve.wait_ge(x_loaded[par], 16 * (u // 2) + 16)

            def wait_stats1(u):
                dve.wait_ge(stats1_done, UB * (u + 1))

            def wait_x1(u):
                dve.wait_ge(x1_done, u + 1)

            def wait_stats2(u):
                dve.wait_ge(stats2_done, UB * (u + 1))

            def front_stats(u, par):
                stats(u, stats1, stats1_done)

            def front_norm(u, par):
                dve.wait_ge(rstd1_done, u + 1)
                if not first(u):
                    dve.wait_ge(xT_ps, u)
                for b in range(UB):
                    dve.tensor_scalar(xhat[:, b, :], x_all[:, bass.ds(u * UB + b, 1), :].rearrange("p o d -> p (o d)"),
                                      mv1[:, b, 0:1], rstd1[:, b:b + 1], ALU.subtract, ALU.mult).then_inc(xhat_done, 1)

            def front_qk(u, par):
                for m, (ps, dst, bone) in enumerate(((bank[0], qT[par], bq_one), (bank[1], kT, bk_one))):
                    dve.wait_ge(exp_done, 2 * u + m + 1)
                    dve.scalar_tensor_tensor(dst[:], ps[:], bone[:], expn[:, m, :], ALU.add, ALU.max).then_inc(qk_done, 1)
                dve.wait_ge(qk_done, 2 * u + 2)
                kv = kT[:].rearrange("p (c s) -> p c s", s=CH)
                for j in range(4):
                    dve.tensor_scalar(Kexp[par][:, :, j, :], kv, headmask[:, j:j + 1], None, ALU.mult).then_inc(kexp_done, 1)

            def front_v(u, par):
                dve.wait_ge(v_ps, u + 1)
                for half in range(2):
                    ps = bank[2 + half]
                    for a in range(2):
                        rows = slice(a * CH, a * CH + CH)
                        cs = slice(half * NCH // 2, (half + 1) * NCH // 2)
                        src = ps[rows, :].rearrange("p (x j a k) -> p x j a k", j=2, a=2, k=HD)[:, :, :, a, :]
                        dst = Vexp[par][rows, cs].rearrange("p c r j (i a k) -> p (c r) j i a k", i=2, a=2)
                        for j in range(2):
                            bvv = bv_b[rows, :].rearrange("p (r j a k) -> p r j a k", r=RG, j=2, a=2)[:, :, j, a, :]
                            dve.tensor_tensor(
                                dst[:, :, j, j, a, :].rearrange("p (c r) k -> p c r k", r=RG),
                                src[:, :, j, :].rearrange("p (c r) k -> p c r k", r=RG),
                                bvv.unsqueeze(1).to_broadcast([CH, NCH // 2, RG, HD]), ALU.add).then_inc(vexp_done, 1)
                    dve.tensor_tensor(Vtok[:, 2 * half:2 * half + 2, :],
                                      ps[0:CH, :].rearrange("p (b c k) -> p b c k", b=2, c=2)[:, :, 0, :],
                                      bv_b[0:CH, :].unsqueeze(1).to_broadcast([CH, 2, P]), ALU.add).then_inc(vexp_done, 1)

            def front_z(u, par):
                for b in range(UB):
                    cols = slice(b * L, (b + 1) * L)
                    dve.tensor_tensor_scan(Z[:, cols], ones[:], qT[par][:, cols], 0.0, ALU.mult, ALU.add).then_inc(z_done, 1)
                dve.wait_ge(z_done, UB * (u + 1))
                dve.reciprocal(rZ[par][:], Z[:]).then_inc(rz_done, 1)

            def front_state(u, par):
                dve.wait_ge(state_ps, u + 1)
                dve.tensor_tensor(state[par][:], bank[1][:].rearrange("p (b k) -> p b k", b=UB),
                                  blockdiag[:].unsqueeze(1).to_broadcast([P, UB, P]), ALU.mult).then_inc(state_done, 1)

            def mask_scores(u, t):
                dve.wait_ge(scores_ps, NBLK * u + t + 1)
                if t >= 4:
                    dve.wait_ge(av_done, NBLK * u + t - 3)
                dve.tensor_tensor(Pm[:, t % 4, :].rearrange("p (n t) -> p n t", t=CH),
                                  bank[4 + t % 2][:].rearrange("p (n t) -> p n t", t=CH),
                                  causal[:].unsqueeze(1).to_broadcast([P, UT // CH, CH]), ALU.mult).then_inc(p_done, 1)

            def tail_o(u, par):
                dve.wait_ge(av_done, NBLK * (u + 1))
                dve.wait_ge(rz_done, u + 1)
                dve.tensor_tensor(oT[:], bank[6][:], rZ[par][:], ALU.mult).then_inc(o_done, 1)

            def tail_x1(u):
                dve.wait_ge(ao_ps, u + 1)
                dve.wait_ge(xb_done, u + 1)
                xu = x_all[:, bass.ds(u * UB, UB), :]
                dve.tensor_tensor(xu, bank[7][:].rearrange("p (b d) -> p b d", b=UB), xu, ALU.add).then_inc(x1_done, 1)

            def tail_norm(u, par):
                dve.wait_ge(rstd2_done, u + 1)
                for b in range(UB):
                    dve.tensor_scalar(x2hat[par][:, b, :], x_all[:, bass.ds(u * UB + b, 1), :].rearrange("p o d -> p (o d)"),
                                      mv2[:, b, 0:1], rstd2[:, b:b + 1], ALU.subtract, ALU.mult).then_inc(x2hat_done, 1)

            ROUTER = 12

            def tail_bids(u):
                dve.wait_ge(lg_ps, u + 1)
                lg = bank[7][:, 0:UB * E].rearrange("p (b e) -> p b e", b=UB)
                dve.tensor_tensor(conf[:], lg, cb_b[:].unsqueeze(1).to_broadcast([P, UB, E]), ALU.add).then_inc(lg_done, 1)

            def tail_choose(u):
                step = [ROUTER * u]

                def done(ins, wait=True):
                    ins.then_inc(router, 1)
                    step[0] = step[0] + 1
                    if wait:
                        dve.wait_ge(router, step[0])

                dve.wait_ge(lg_exp, u + 1)
                done(dve.tensor_scalar(conf[:], conf_e[:], 1.0, None, ALU.add))
                done(dve.reciprocal(conf_e[:], conf[:]))
                done(dve.tensor_tensor(bids[:], conf_e[:], wealth_b[:].unsqueeze(1).to_broadcast([P, UB, E]), ALU.mult))
                dve.memset(carrier[:], 0.0)
                for b in range(UB):
                    dve.max(top[:, b, :], bids[:, b, :]).then_inc(top_done, 1)
                dve.wait_ge(top_done, UB * (u + 1))
                dve.tensor_tensor(vdiff[:], top[:, :, 1], top[:, :, 0], ALU.subtract).then_inc(vdiff_done, 1)
                for b in range(UB):
                    done(dve.max_index(topi[:, b, :], top[:, b, :], bids[:, b, :]), wait=(b == UB - 1))
                for s in range(TOP):
                    done(dve.tensor_tensor(hot[:, s], iota8[:].unsqueeze(1).to_broadcast([P, UB, E]),
                                           topi[:, :, s:s + 1].to_broadcast([P, UB, E]), ALU.is_equal), wait=(s == 1))
                done(dve.tensor_tensor(chosen[:], hot[:, 0], hot[:, 1], ALU.add))
                dve.wait_ge(vexp_act, u + 1)
                done(dve.tensor_scalar(vdiff[:], vexp[:], 1.0, None, ALU.add))
                done(dve.reciprocal(wts[:], vdiff[:]))
                if not first(u):
                    dve.wait_ge(dispatched, 16 * UB * TOP * u)
                dve.tensor_scalar(token_rows[:, :, 0, D], wts[:], 1.0 / WSCALE, None, ALU.mult).then_inc(weights_done, 1)
                dve.scalar_tensor_tensor(token_rows[:, :, 1, D], wts[:], 1.0 / WSCALE, vexp[:], ALU.mult, ALU.mult).then_inc(weights_done, 1)

            def tail_place(u):
                dve.wait_ge(rank_ps, u + 1)
                dve.tensor_tensor(rank[:], bank[7][:, 64:64 + UB * E].rearrange("p (b e) -> p b e", b=UB),
                                  region[:].unsqueeze(1).to_broadcast([P, UB, E]), ALU.add).then_inc(placing, 1)
                dve.tensor_reduce(chosen_sum[:], chosen[:].rearrange("p b e -> p e b"), AX_X, ALU.add).then_inc(placing, 1)
                dve.wait_ge(placing, 3 * u + 2)
                dve.tensor_tensor(place[:], hot[:], rank[:].unsqueeze(1).to_broadcast([P, TOP, UB, E]), ALU.mult).then_inc(placing, 1)
                dve.tensor_tensor(before[:], before[:], chosen_sum[:], ALU.add).then_inc(before_done, 1)
                dve.wait_ge(placing, 3 * u + 3)
                with nc.allow_low_precision(reason="a row's number is a whole number, exact in any of the types"):
                    dve.tensor_reduce(rows_to[:], place[:], AX_X, ALU.add).then_inc(rows_to_done, 1)

            def weights(u, m):
                dve.wait_ge(whi_done, 3 * u + m + 1)
                cols = bass.ds(u * (3 * I) + m * I, I)
                dve.scalar_tensor_tensor(w_lo[:, cols], bank[2 + m % 2][:], WSCALE, w_hi[:, cols], ALU.mult, ALU.subtract).then_inc(wlo_done, 1)

            def body(u, par):
                if not first(u):
                    tail_o(u - 1, 1 - par)
                if not last(u):
                    wait_x(u + 1, 1 - par)
                mask_scores(u, 1)
                if not last(u):
                    front_stats(u + 1, 1 - par)
                if not first(u):
                    tail_x1(u - 1)
                weights(u, 0)
                if not last(u):
                    wait_stats1(u + 1)
                if not first(u):
                    wait_x1(u - 1)
                mask_scores(u, 2)
                if not last(u):
                    aggregate(mv1, stats1, mv1_done)
                if not first(u):
                    stats(u - 1, stats2, stats2_done)
                weights(u, 1)
                if not last(u):
                    front_norm(u + 1, 1 - par)
                if not first(u):
                    wait_stats2(u - 1)
                mask_scores(u, 3)
                if not first(u):
                    aggregate(mv2, stats2, mv2_done)
                mask_scores(u, 4)
                if not first(u):
                    tail_norm(u - 1, 1 - par)
                weights(u, 2)
                mask_scores(u, 5)
                if not last(u):
                    front_qk(u + 1, 1 - par)
                mask_scores(u, 6)
                if not last(u):
                    front_v(u + 1, 1 - par)
                if not first(u):
                    tail_bids(u - 1)
                mask_scores(u, 7)
                if not first(u):
                    tail_choose(u - 1)
                if not last(u):
                    front_state(u + 1, 1 - par)
                    front_z(u + 1, 1 - par)
                    mask_scores(u + 1, 0)
                if not first(u):
                    tail_place(u - 1)

            dve.wait_ge(const_loaded, 16 * N_LOADS)
            dve.wait_ge(const_made, N_MADE)
            for b_c, b_n, b_1 in ((bq_c, bq_neg, bq_one), (bk_c, bk_neg, bk_one)):
                dve.tensor_scalar(b_n[:], b_c[:], -1.0, None, ALU.mult).then_inc(const_dve, 1)
                dve.tensor_scalar(b_1[:], b_c[:], 1.0, None, ALU.add).then_inc(const_dve, 1)
            dve.tensor_reduce(headmask[:], headsel[:].rearrange("p r j -> p j r"), AX_X, ALU.add).then_inc(const_dve, 1)
            dve.wait_ge(confT_ps, 1)
            dve.tensor_copy(confT[:], bank[7][:, 0:E]).then_inc(const_dve, 1)
            dve.wait_ge(const_dve, 6)
            wait_x(0, 0)
            front_stats(0, 0)
            wait_stats1(0)
            aggregate(mv1, stats1, mv1_done)
            front_norm(0, 0)
            front_qk(0, 0)
            front_v(0, 0)
            front_z(0, 0)
            front_state(0, 0)
            mask_scores(0, 0)
            steady(Units(dve, body))
            tail_o(UNITS - 1, (UNITS - 1) % 2)
            tail_x1(UNITS - 1)
            wait_x1(UNITS - 1)
            stats(UNITS - 1, stats2, stats2_done)
            wait_stats2(UNITS - 1)
            aggregate(mv2, stats2, mv2_done)
            tail_norm(UNITS - 1, (UNITS - 1) % 2)
            tail_bids(UNITS - 1)
            tail_choose(UNITS - 1)
            tail_place(UNITS - 1)

            n_table = [0]

            def entry(ins):
                ins.then_inc(table, 1)
                n_table[0] += 1
                dve.wait_ge(table, n_table[0])

            dve.wait_ge(count_ps, 1)
            entry(dve.tensor_copy(count[:], bank[7][0:1, 96:96 + E]))
            dve.tensor_tensor(pad_at[:], count[:], region[0:1, :], ALU.add).then_inc(pad_at_done, 1)
            entry(dve.tensor_scalar(blocks_u[:], count[:], float(P - 1), None, ALU.add))
            entry(dve.tensor_scalar(blocks_s[:], blocks_u[:], P.bit_length() - 1, None, ALU.logical_shift_right))
            entry(dve.tensor_copy(blocks[:], blocks_s[:]))
            entry(dve.tensor_tensor_scan(blocks_to[:], ones[0:1, 0:E], blocks[:], 0.0, ALU.mult, ALU.add))
            entry(dve.tensor_tensor(passed[:], tile_no[:].unsqueeze(2).to_broadcast([1, TILES, E]),
                                    blocks_to[:].unsqueeze(1).to_broadcast([1, TILES, E]), ALU.is_ge))
            entry(dve.tensor_reduce(tile_expert[:], passed[:], AX_X, ALU.add))
            entry(dve.tensor_tensor(passed_blocks[:], passed[:], blocks[:].unsqueeze(1).to_broadcast([1, TILES, E]), ALU.mult))
            entry(dve.tensor_reduce(tile_start[:], passed_blocks[:], AX_X, ALU.add))
            entry(dve.tensor_tensor(tile_start[:], tile_no[:], tile_start[:], ALU.subtract))
            entry(dve.tensor_scalar(tile_start[:], tile_start[:], float(P), None, ALU.mult))
            entry(dve.scalar_tensor_tensor(tile_row[:], tile_expert[:], float(REGION), tile_start[:], ALU.mult, ALU.add))
            entry(dve.tensor_scalar(row_at[:], tile_row[:], float(E * REGION), None, ALU.min))
            entry(dve.tensor_scalar(tile_row[:], tile_expert[:], float(E - 1), None, ALU.min))
            entry(dve.tensor_scalar(col_at[:], tile_row[:], float(3 * I), None, ALU.mult))
            assert n_table[0] == TABLE, n_table[0]

            def copy_T(i, k):
                dve.wait_ge(xgT_ps, i + 1)
                if at_least(i, 2):
                    dve.wait_ge(up_ps, i - 1)
                dve.tensor_copy(xgT[:, k % 2, :], bank[4 + k % 2][:, 0:P].bitcast(F16)).then_inc(xgT_copied, 1)

            def tile_step(i, k):
                dve.wait_ge(silu_done, i + 1)
                dve.wait_ge(up_ps, i + 1)
                dve.scalar_tensor_tensor(hid[:, k % 2, :], bank[2 + k % 2][:], 1.0 / WSCALE, silu[:, k % 2, :],
                                         ALU.mult, ALU.mult).then_inc(hid_done, 1)
                if before_end(i, TILES - 2):
                    copy_T(i + 2, k + 2)
                dve.wait_ge(hi_done, i + 1)
                dve.tensor_tensor(hid_lo[:, k % 2, :], hid[:, k % 2, :], hid_hi[:, k % 2, :], ALU.subtract).then_inc(lo_done, 1)

            copy_T(0, 0)
            copy_T(1, 1)
            tiles(dve, tile_step)

            for u in range(UNITS):
                dve.wait_ge(y_loaded[u], 16)
                xu = x_all[:, u * UB:(u + 1) * UB, :]
                dve.tensor_tensor(xu, xu, y_back[u % 2][:, u // 2, :, 0, :], ALU.add).then_inc(sum_done, 1)
                dve.wait_ge(sum_done, u + 1)
                dve.tensor_tensor(xu, xu, y_back[u % 2][:, u // 2, :, 1, :], ALU.add).then_inc(out_done, 1)

        @block.tensor
        def _(pe):
            def weights(u, par, m):
                if m == 0:
                    pe.wait_ge(w_loaded[par], 48 * (u // 2) + 48)
                    if not first(u):
                        pe.wait_ge(vexp_done, 10 * (u + 1))
                elif m == 2:
                    pe.wait_ge(wlo_done, 3 * u + 1)
                for c in range(IC):
                    ins = pe.transpose(bank[2 + m % 2][:, c * P:(c + 1) * P], w_raw[par][:, m, c * P:(c + 1) * P], ident[:])
                ins.then_inc(w_ps, 1)

            def front_transposes(u, par):
                pe.wait_ge(xhat_done, UB * (u + 1))
                if not first(u):
                    pe.wait_ge(ktok_copied, u)
                for b in range(UB):
                    ins = pe.transpose(bank[0][:, b * L:(b + 1) * L], xhat[:, b, :], ident[:])
                ins.then_inc(xT_ps, 1)
                pe.wait_ge(ctx_loaded[par], 16 * (u // 2) + 16)
                if not first(u):
                    pe.wait_ge(state_done, u)
                for b in range(UB):
                    ins = pe.transpose(bank[1][:, b * L:(b + 1) * L], ctx_s[par][:, b, :], ident[:])
                ins.then_inc(cT_ps, 1)

            def front_project(u, par):
                pe.wait_ge(xT_copied, u + 1)
                pe.matmul(bank[0][:], Wq_s[:], xT[:], start=True, stop=True).then_inc(q_ps, 1)
                pe.wait_ge(cT_copied, u + 1)
                pe.matmul(bank[1][:], Wk_s[:], cT[:, :, 0, :], start=True, stop=True).then_inc(k_ps, 1)
                if isinstance(u, int) and u == 0:
                    pass
                else:
                    pe.wait_ge(wlo_done, 3 * u)
                for c in range(NCH):
                    ins = pe.matmul(bank[2 + c // 4][:, (c % 4) * P:(c % 4 + 1) * P], cT[:, c, :, :], Wv_s[:], start=True, stop=True)
                ins.then_inc(v_ps, 1)

            def front_ktok(u, par):
                pe.wait_ge(qk_done, 2 * u + 2)
                for b in range(UB):
                    ins = pe.transpose(bank[0][:, b * P:(b + 1) * P], kT[:, b * L:(b + 1) * L], ident[:])
                ins.then_inc(ktok_ps, 1)

            def front_state(u, par):
                pe.wait_ge(ktok_copied, u + 1)
                pe.wait_ge(vexp_done, 10 * (u + 1))
                for b in range(UB):
                    ins = pe.matmul(bank[1][:, b * P:(b + 1) * P], Ktok[:, b, :], Vtok[:, b, :], start=True, stop=True)
                ins.then_inc(state_ps, 1)

            def scores(u, par, t):
                bb, r = t // RG, t % RG
                rows = slice(32 * r, 32 * r + 32)
                if t == 0:
                    pe.wait_ge(kexp_done, 4 * (u + 1))
                if t >= 2:
                    pe.wait_ge(p_done, NBLK * u + t - 1)
                elif not first(u):
                    pe.wait_ge(p_done, NBLK * u + t - 1)
                for n in range(4):
                    c = bb * 4 + n
                    for j in range(2):
                        ins = pe.matmul(bank[4 + t % 2][:, (n * 2 + j) * CH:(n * 2 + j + 1) * CH],
                                        Kexp[par][rows, c, 2 * j:2 * j + 2, :], qT[par][rows, c * CH:(c + 1) * CH],
                                        start=True, stop=True)
                ins.then_inc(scores_ps, 1)

            def values(u, par, t):
                bb, r = t // RG, t % RG
                rows = slice(32 * r, 32 * r + 32)
                if t == 0:
                    pe.wait_ge(state_done, u + 1)
                    if not first(u):
                        pe.wait_ge(o_done, u)
                    for b in range(UB):
                        pe.matmul(bank[6][:, b * L + CH:(b + 1) * L], state[par][:, b, :], qT[par][:, b * L + CH:(b + 1) * L],
                                  start=(b == 0), stop=False, skip_group_check=True)
                pe.wait_ge(p_done, NBLK * u + t + 1)
                for n in range(4):
                    c = bb * 4 + n
                    for j in range(2):
                        ins = pe.matmul(bank[6][rows, c * CH:(c + 1) * CH], Vexp[par][:, c, r, j, :],
                                        Pm[:, t % 4, (n * 2 + j) * CH:(n * 2 + j + 1) * CH],
                                        start=False, stop=(j == 1), skip_group_check=True)
                ins.then_inc(av_done, 1)

            def tail_out(u):
                pe.wait_ge(o_done, u + 1)
                if not first(u):
                    pe.wait_ge(rows_to_done, u)
                for b in range(UB):
                    ins = pe.matmul(bank[7][:, b * P:(b + 1) * P], oT[:, b * L:(b + 1) * L], Wo_s[:], start=True, stop=True)
                ins.then_inc(ao_ps, 1)

            def tail_x2(u, par):
                pe.wait_ge(x2hat_done, UB * (u + 1))
                for b in range(UB):
                    ins = pe.transpose(bank[7][:, b * L:(b + 1) * L], x2hat[par][:, b, :], ident[:])
                ins.then_inc(x2T_ps, 1)

            def tail_logits(u):
                pe.wait_ge(x2T_copied, u + 1)
                for b in range(UB):
                    ins = pe.matmul(bank[7][:, b * E:(b + 1) * E], x2T[:, b * L:(b + 1) * L], confT[:], start=True, stop=True)
                ins.then_inc(lg_ps, 1)

            def tail_rank(u):
                pe.wait_ge(router, 12 * u + 10)
                if not first(u):
                    pe.wait_ge(before_done, u)
                ps = bank[7][:, 64:64 + UB * E]
                pe.matmul(ps, earlier[:], chosen[:].rearrange("p b e -> p (b e)"), start=True, stop=False, skip_group_check=True)
                for b in range(UB - 1):
                    pe.matmul(ps[:, (b + 1) * E:].rearrange("p (n e) -> p n e", e=E), ones_b[:],
                              chosen[:, b:b + 1, :].to_broadcast([P, UB - 1 - b, E]), start=False, stop=False, skip_group_check=True)
                pe.matmul(ps.rearrange("p (b e) -> p b e", b=UB), ones_b[:], before[:].unsqueeze(1).to_broadcast([P, UB, E]),
                          start=False, stop=True, skip_group_check=True).then_inc(rank_ps, 1)

            def body(u, par):
                if not first(u):
                    tail_out(u - 1)
                weights(u, par, 0)
                values(u, par, 0)
                scores(u, par, 2)
                weights(u, par, 1)
                values(u, par, 1)
                scores(u, par, 3)
                if not last(u):
                    front_transposes(u + 1, 1 - par)
                values(u, par, 2)
                scores(u, par, 4)
                weights(u, par, 2)
                values(u, par, 3)
                scores(u, par, 5)
                if not first(u):
                    tail_x2(u - 1, 1 - par)
                if not last(u):
                    front_project(u + 1, 1 - par)
                values(u, par, 4)
                scores(u, par, 6)
                if not first(u):
                    tail_logits(u - 1)
                values(u, par, 5)
                scores(u, par, 7)
                if not last(u):
                    front_ktok(u + 1, 1 - par)
                values(u, par, 6)
                values(u, par, 7)
                if not last(u):
                    front_state(u + 1, 1 - par)
                    scores(u + 1, 1 - par, 0)
                    scores(u + 1, 1 - par, 1)
                if not first(u):
                    tail_rank(u - 1)

            pe.wait_ge(const_made, N_MADE)
            pe.wait_ge(const_loaded, 16 * N_LOADS)
            pe.transpose(bank[7][:, 0:E], conf_s[:], ident[0:E, 0:E]).then_inc(confT_ps, 1)
            front_transposes(0, 0)
            front_project(0, 0)
            front_ktok(0, 0)
            front_state(0, 0)
            scores(0, 0, 0)
            scores(0, 0, 1)
            steady(Units(pe, body))
            tail_out(UNITS - 1)
            tail_x2(UNITS - 1, (UNITS - 1) % 2)
            tail_logits(UNITS - 1)
            tail_rank(UNITS - 1)
            pe.wait_ge(before_done, UNITS)
            pe.matmul(bank[7][:, 96:96 + E], ones_b[:], before[:], start=True, stop=True).then_inc(count_ps, 1)

            def transposes(i, k):
                pe.wait_ge(xg_loaded[k % 4], 16 * (i // 4) + 16)
                if at_least(i, 2):
                    pe.wait_ge(xgT_copied, i - 1)
                for half in range(2):
                    ins = pe.transpose(bank[4 + k % 2][:, half * (P // 2):(half + 1) * (P // 2)].bitcast(F16),
                                       xg_halves[:, k % 4, half * P:(half + 1) * P], ident_h[:])
                ins.then_inc(xgT_ps, 1)

            def gate_up(i, k):
                col = pe.value_load(col_at[0:1, bass.ds(i, 1)], min_val=0, max_val=(E - 1) * 3 * I)
                pe.wait_ge(xgT_copied, i + 1)
                if at_least(i, 2):
                    pe.wait_ge(hid_done, i - 1)
                x_hi, x_lo = xgT[:, k % 2, 0:P], xgT[:, k % 2, P:2 * P]
                for m, ready in ((0, gate_ps), (1, up_ps)):
                    for c in range(IC):
                        ps = bank[2 * m + k % 2][:, c * P:(c + 1) * P]
                        w = bass.ds(col + (m * I + c * P), P)
                        pe.matmul(ps, w_hi[:, w], x_hi, start=(c == 0), stop=False, skip_group_check=True)
                        pe.matmul(ps, w_hi[:, w], x_lo, start=False, stop=False, skip_group_check=True)
                        ins = pe.matmul(ps, w_lo[:, w], x_hi, start=False, stop=True, skip_group_check=True)
                    ins.then_inc(ready, 1)

            def down(i, k):
                col = pe.value_load(col_at[0:1, bass.ds(i, 1)], min_val=0, max_val=(E - 1) * 3 * I)
                pe.wait_ge(lo_done, i + 1)
                if at_least(i, 2):
                    pe.wait_ge(y_done, i - 1)
                ps = bank[6 + k % 2][:, 0:P]
                for c in range(IC):
                    h = slice(c * P, (c + 1) * P)
                    w = bass.ds(col + (2 * I + c * P), P)
                    pe.matmul(ps, hid_hi[:, k % 2, h], w_hi[:, w], start=(c == 0), stop=False)
                    pe.matmul(ps, hid_hi[:, k % 2, h], w_lo[:, w], start=False, stop=False)
                    ins = pe.matmul(ps, hid_lo[:, k % 2, h], w_hi[:, w], start=False, stop=(c == IC - 1))
                ins.then_inc(y_ps, 1)

            def tile_step(i, k):
                if before_end(i):
                    gate_up(i, k)
                if before_end(i, TILES - 2):
                    transposes(i + 2, k + 2)
                if at_least(i, 2):
                    down(i - 2, (k - 2) % 4)

            pe.wait_ge(wlo_done, 3 * E)
            pe.wait_ge(table, TABLE)
            transposes(0, 0)
            transposes(1, 1)
            tiles(pe, tile_step, 2)


_INS = ['x', 'ctx_1024', 'L0_xattn_Wq', 'L0_xattn_bq', 'L0_xattn_Wk', 'L0_xattn_bk', 'L0_xattn_Wv', 'L0_xattn_bv',
        'L0_xattn_Wo', 'L0_xattn_bo', 'L0_ffn_conf_w', 'L0_ffn_conf_b', 'L0_ffn_gate_w', 'L0_ffn_up_w',
        'L0_ffn_down_w', 'L0_ffn_wealth']


def kernel(**inputs):
    import numpy as _np
    import concourse.bacc as _bacc
    from concourse import mybir as _mybir
    from concourse.bass_utils import run_bass_kernel_spmd as _run

    nc = _bacc.Bacc("TRN2", target_bir_lowering=False, num_devices=1)
    arrays, args = {}, []
    for name in _INS:
        a = _np.ascontiguousarray(inputs[name])
        arrays[f"in_{name}_dram"] = a
        args.append(nc.dram_tensor(f"in_{name}_dram", a.shape, _mybir.dt.from_np(a.dtype), kind="ExternalInput").ap())
    shape = arrays["in_x_dram"].shape
    args.append(nc.dram_tensor("out_dram", shape, _mybir.dt.float32, kind="ExternalOutput").ap())
    attention_moe_kernel(nc, *args)
    r = _run(nc, [arrays], core_ids=[0])
    return r.results[0]["out_dram"]
```

```python
from contextlib import ExitStack

import concourse.bass as bass
from concourse import mybir

ALU = mybir.AluOpType
ACT = mybir.ActivationFunctionType
AX_X = mybir.AxisListType.X
F32 = mybir.dt.float32
F16 = mybir.dt.float16
BF16 = mybir.dt.bfloat16
U32 = mybir.dt.uint32
I32 = mybir.dt.int32

P = 128
WSCALE = 64.0
KSCALE = 16.0
EPS = 1e-5


def attention_moe_kernel(nc, x, ctx_in, Wq, bq, Wk, bk, Wv, bv, Wo, bo,
                         conf_w, conf_b, gate_w, up_w, down_w, wealth, out):
    NB, L, D = x.shape
    E, I, _ = gate_w.shape
    H, HD = 16, D // 16
    UB = 4
    UNITS = NB // UB
    UT = UB * L
    CH = 64
    NCH = UB * L // CH
    RG = 4
    NBLK = 2 * RG
    IC = I // P
    HC = IC // 2
    TOP = 2
    NT = NB * L
    TB = 2
    TT = TB * P
    REGION = NT + TT
    ROW = D + 2
    TILES = (NT * TOP + E * (TT - 1)) // TT
    SLOTS = -(-TILES // 4) * 4
    FAR = 4.0 * NT
    assert L == P and D == P and E == UNITS and HD == 8 and L == 2 * CH

    with ExitStack() as ctx:
        def sb(name, shape, dt=F32):
            return ctx.enter_context(nc.sbuf_tensor(name, shape, dt))

        def sem(name):
            return ctx.enter_context(nc.semaphore(name))

        ident = sb("ident", [P, P])
        causal = sb("causal", [P, CH])
        headmask = sb("headmask", [P, 4])
        headsel = sb("headsel", [P, RG, 4])
        blockdiag = sb("blockdiag", [P, P])
        ones = sb("ones", [P, P])
        minus_half = sb("minus_half", [P, UB])
        zero = sb("zero", [P, UB])
        eps = sb("eps", [P, UB])
        carrier = sb("carrier", [P, 5])
        iota8 = sb("iota8", [P, E])
        Wq_s, Wk_s, Wv_s, Wo_s = (sb(n, [P, P]) for n in ("Wq_s", "Wk_s", "Wv_s", "Wo_s"))
        bq_c, bk_c = sb("bq_c", [P, 1]), sb("bk_c", [P, 1])
        bq_neg, bk_neg = sb("bq_neg", [P, 1]), sb("bk_neg", [P, 1])
        bq_one, bk_one = sb("bq_one", [P, 1]), sb("bk_one", [P, 1])
        bv_b, bo_b = sb("bv_b", [P, P]), sb("bo_b", [P, P])
        cb_b, wealth_b = sb("cb_b", [P, E]), sb("wealth_b", [P, E])
        conf_s = sb("conf_s", [E, P])
        confT = sb("confT", [P, E])
        x_all = sb("x_all", [P, NB, P])
        ctx_s = [sb(f"ctx_s{i}", [P, UB, P]) for i in range(2)]
        stats1 = sb("stats1", [P, UB, 6])
        mv1 = sb("mv1", [P, UB, 2])
        ve1 = sb("ve1", [P, UB])
        nm1 = sb("nm1", [P, UB])
        rstd1 = sb("rstd1", [P, UB])
        shift1 = sb("shift1", [P, UB])
        xhat = sb("xhat", [P, UB, P])
        xT = sb("xT", [P, UT])
        cT = sb("cT", [P, NCH, 2, CH])
        expn = sb("expn", [P, 2, UT])
        qT = [sb(f"qT{i}", [P, UT]) for i in range(2)]
        kT = sb("kT", [P, UT])
        q_hi, q_lo = ([sb(f"{n}{i}", [P, UT], F16) for i in range(2)] for n in ("q_hi", "q_lo"))
        k_hi, k_lo = (sb(n, [P, UT], F16) for n in ("k_hi", "k_lo"))
        k_scaled, q_scaled = (sb(n, [P, UT]) for n in ("k_scaled", "q_scaled"))
        Khi, Klo = ([sb(f"{n}{i}", [P, NCH, 4, CH], F16) for i in range(2)] for n in ("Khi", "Klo"))
        Vexp = [sb(f"Vexp{i}", [P, NCH, RG, 2, 32]) for i in range(2)]
        Vtok = sb("Vtok", [CH, UB, P])
        Ktok = sb("Ktok", [CH, UB, P])
        state = [sb(f"state{i}", [P, UB, P]) for i in range(2)]
        Z = sb("Z", [P, UT])
        Pm = sb("Pm", [P, 4, UT])
        oT = sb("oT", [P, UT])
        stats2 = sb("stats2", [P, UB, 6])
        mv2 = sb("mv2", [P, UB, 2])
        ve2 = sb("ve2", [P, UB])
        nm2 = sb("nm2", [P, UB])
        rstd2 = sb("rstd2", [P, UB])
        shift2 = sb("shift2", [P, UB])
        x2hat = [sb(f"x2hat{i}", [P, UB, P]) for i in range(2)]
        x2T = sb("x2T", [P, UT])
        conf = sb("conf", [P, UB, E])
        conf_e = sb("conf_e", [P, UB, E])
        bids = sb("bids", [P, UB, E])
        top = sb("top", [P, UB, 8])
        topi = sb("topi", [P, UB, 8], U32)
        vdiff = sb("vdiff", [P, UB])
        vexp = sb("vexp", [P, UB])
        wts = sb("wts", [P, UB])
        hot = sb("hot", [P, TOP, UB, E])
        chosen = sb("chosen", [P, UB, E], BF16)
        chosen_sum = sb("chosen_sum", [P, E])
        before = sb("before", [P, E], BF16)
        earlier = sb("earlier", [P, P], BF16)
        ones_b = sb("ones_b", [P, P], BF16)
        region = sb("region", [P, E])
        rank = sb("rank", [P, UB, E])
        place = sb("place", [P, TOP, UB, E])
        rows_to = sb("rows_to", [P, TOP, UB], U32)
        pair_id = sb("pair_id", [P, UB, TOP])
        unit_ids = sb("unit_ids", [P, UB, TOP])
        unit_start = sb("unit_start", [P, UB, TOP])
        token_rows = sb("token_rows", [P, UB, TOP, ROW])
        row_halves = token_rows[:].rearrange("p b s r -> p (b s r)").bitcast(F16).rearrange("p (b s r) -> p b s r", b=UB, s=TOP)
        pad_row = sb("pad_row", [P, ROW])
        ident_h = sb("ident_h", [P, P], F16)
        tile_no = sb("tile_no", [1, SLOTS])
        count = sb("count", [1, E])
        pad_at = sb("pad_at", [1, E], I32)
        blocks_u = sb("blocks_u", [1, E], U32)
        blocks_s = sb("blocks_s", [1, E], U32)
        blocks = sb("blocks", [1, E])
        blocks_to = sb("blocks_to", [1, E])
        passed = sb("passed", [1, SLOTS, E])
        passed_blocks = sb("passed_blocks", [1, SLOTS, E])
        tile_expert = sb("tile_expert", [1, SLOTS])
        tile_start = sb("tile_start", [1, SLOTS])
        tile_row = sb("tile_row", [1, SLOTS])
        row_at = sb("row_at", [1, SLOTS], I32)
        expert_of = sb("expert_of", [1, SLOTS + 4])
        packed = sb("packed", [1, SLOTS // 4])
        experts_at = sb("experts_at", [1, SLOTS // 4], I32)
        w_raw = [sb(f"w_raw{i}", [P, 3, IC * P]) for i in range(2)]
        W = 3 * IC * P
        w_hi = sb("w_hi", [P, E * W], F16)
        w_lo = sb("w_lo", [P, E * W], F16)
        xg = sb("xg", [P, 4, TB, ROW])
        xg_halves = xg[:].rearrange("p k s r -> p (k s r)").bitcast(F16).rearrange("p (k s r) -> p k s r", k=4, s=TB)
        xgT = sb("xgT", [P, 2, 2, TT], F16)
        y_to = sb("y_to", [P, 4, TB], U32)
        y_scale = sb("y_scale", [P, 4, TB])
        silu = sb("silu", [P, 2, HC * TT])
        silu_warm = sb("silu_warm", [P, 1])
        hid = sb("hid", [P, 2, HC * TT])
        hid_hi = sb("hid_hi", [P, 2, 2, HC * TT], F16)
        hid_lo = Klo[0][:].rearrange("p c j s -> p (c j s)").rearrange("p (k q t) -> p k q t", k=2, q=2)
        y_sb = sb("y_sb", [P, 4, TB, P])
        BACK = UNITS // 2 * UB * TOP * P
        y_back = [w[:, 0:2 * BACK].bitcast(F32).rearrange("p (u b s d) -> p u b s d", u=UNITS // 2, b=UB, s=TOP)
                  for w in (w_hi, w_lo)]

        by_expert = nc.dram_tensor("by_expert", (E * REGION + TT, ROW), F32, kind="Internal").ap()
        by_token = nc.dram_tensor("by_token", (NT * TOP, D), F32, kind="Internal").ap()

        bank = [ctx.enter_context(nc.psum_tensor(f"bank{i}", [P, 512], F32)) for i in range(8)]

        qk_loaded = sem("qk_loaded")
        const_loaded = sem("const_loaded")
        const_made = sem("const_made")
        const_dve = sem("const_dve")
        confT_ps = sem("confT_ps")
        x_loaded = [sem(f"x_loaded{i}") for i in range(2)]
        ctx_loaded = [sem(f"ctx_loaded{i}") for i in range(2)]
        w_loaded = [sem(f"w_loaded{i}") for i in range(2)]
        stats1_done = sem("stats1_done")
        mv1_done = sem("mv1_done")
        ve1_done = sem("ve1_done")
        rstd1_done = sem("rstd1_done")
        shift1_done = sem("shift1_done")
        xhat_done = sem("xhat_done")
        xb_done = sem("xb_done")
        xT_ps = sem("xT_ps")
        cT_ps = sem("cT_ps")
        xT_copied = sem("xT_copied")
        cT_copied = sem("cT_copied")
        q_ps = sem("q_ps")
        k_ps = sem("k_ps")
        v_ps = sem("v_ps")
        neg_done = sem("neg_done")
        exp_done = sem("exp_done")
        qk_done = sem("qk_done")
        qkhi_done = sem("qkhi_done")
        kmask_hi_done = sem("kmask_hi_done")
        kmask_lo_done = sem("kmask_lo_done")
        qkscaled_done = sem("qkscaled_done")
        qklo_done = sem("qklo_done")
        vexp_done = sem("vexp_done")
        ktok_ps = sem("ktok_ps")
        ktok_copied = sem("ktok_copied")
        state_ps = sem("state_ps")
        state_done = sem("state_done")
        z_done = sem("z_done")
        scores_ps = sem("scores_ps")
        p_done = sem("p_done")
        av_done = sem("av_done")
        o_done = sem("o_done")
        rz_done = sem("rz_done")
        ao_ps = sem("ao_ps")
        x1_done = sem("x1_done")
        stats2_done = sem("stats2_done")
        mv2_done = sem("mv2_done")
        ve2_done = sem("ve2_done")
        rstd2_done = sem("rstd2_done")
        shift2_done = sem("shift2_done")
        x2hat_done = sem("x2hat_done")
        x2T_ps = sem("x2T_ps")
        x2T_copied = sem("x2T_copied")
        row_hi_done = sem("row_hi_done")
        row_lo_done = sem("row_lo_done")
        row_id_done = sem("row_id_done")
        id_next = sem("id_next")
        lg_ps = sem("lg_ps")
        lg_done = sem("lg_done")
        lg_exp = sem("lg_exp")
        router = sem("router")
        top_done = sem("top_done")
        vdiff_done = sem("vdiff_done")
        vexp_act = sem("vexp_act")
        weights_done = sem("weights_done")
        rank_ps = sem("rank_ps")
        placing = sem("placing")
        before_done = sem("before_done")
        rows_to_done = sem("rows_to_done")
        dispatched = sem("dispatched")
        padded = sem("padded")
        count_ps = sem("count_ps")
        pad_at_done = sem("pad_at_done")
        table = sem("table")
        w_ps = sem("w_ps")
        whi_done = sem("whi_done")
        wlo_done = sem("wlo_done")
        xg_loaded = [sem(f"xg_loaded{i}") for i in range(4)]
        xgT_ps = sem("xgT_ps")
        xgT_copied = sem("xgT_copied")
        y_to_done = sem("y_to_done")
        gate_ps = sem("gate_ps")
        up_ps = sem("up_ps")
        silu_done = sem("silu_done")
        hid_done = sem("hid_done")
        hi_done = sem("hi_done")
        lo_done = sem("lo_done")
        y_ps = sem("y_ps")
        y_done = sem("y_done")
        y_stored = [sem(f"y_stored{i}") for i in range(4)]
        y_loaded = [sem(f"y_loaded{i}") for i in range(UNITS)]
        sum_done = sem("sum_done")
        out_done = sem("out_done")
        stored = sem("stored")

        block = ctx.enter_context(nc.Block())


        x_tok = x.rearrange("b t d -> t b d")
        ctx_tok = ctx_in.rearrange("b t d -> t b d")
        out_tok = out.rearrange("b t d -> t b d")
        N_LOADS = 7
        TABLE = 19
        ROWS_AT = 13
        N_MADE = 24

        def units(engine, body):
            body(0, 0)
            with engine.Fori(0, (UNITS - 2) // 2) as i:
                body(i * 2 + 1, 1)
                body(i * 2 + 2, 0)
            body(UNITS - 1, (UNITS - 1) % 2)

        def tiles(engine, step, ahead=0):
            for i in range(4):
                step(i, i)
            with engine.Fori(0, SLOTS // 4 - 2) as n:
                for k in range(4):
                    step(n * 4 + (4 + k), k)
            for i in range(SLOTS - 4, TILES + ahead):
                step(i, i % 4)

        def at_least(i, n):
            return not isinstance(i, int) or i >= n

        def before_end(i, n=TILES):
            return not isinstance(i, int) or i < n

        def first(u):
            return isinstance(u, int) and u == 0

        def last(u):
            return isinstance(u, int) and u == UNITS - 1

        @block.sync
        def _(sp):
            def load_unit(u, par):
                if not (isinstance(u, int) and u < 2):
                    sp.wait_ge(x_loaded[par], 16 * ((u - par) // 2) if isinstance(u, int) else 16 * (u // 2))
                sp.dma_start(x_all[:, bass.ds(u * UB, UB), :], x_tok[:, bass.ds(u * UB, UB), :]).then_inc(x_loaded[par], 16)
                if not (isinstance(u, int) and u < 2):
                    sp.wait_ge(cT_ps, u - 1)
                sp.dma_start(ctx_s[par][:], ctx_tok[:, bass.ds(u * UB, UB), :]).then_inc(ctx_loaded[par], 16)

            def load_w(u, par):
                if not (isinstance(u, int) and u < 2):
                    sp.wait_ge(w_ps, 3 * (u - 1))
                for m, w in enumerate((gate_w, up_w)):
                    sp.dma_start(w_raw[par][:, m, :].rearrange("p (c h) -> p c h", c=IC),
                                 w[bass.ds(u, 1), :, :].rearrange("o (c p) h -> p (o c) h", p=P)).then_inc(w_loaded[par], 16)
                sp.dma_start(w_raw[par][:, 2, :],
                             down_w[bass.ds(u, 1), :, :].rearrange("o h i -> h (o i)")).then_inc(w_loaded[par], 16)

            load_unit(0, 0)
            for dst, src in ((bk_c, bk), (bq_c, bq)):
                sp.dma_start(dst[:], src.unsqueeze(1)).then_inc(qk_loaded, 16)
            for dst, src in ((Wk_s, Wk), (Wq_s, Wq)):
                sp.dma_start(dst[:], src).then_inc(qk_loaded, 16)
            for dst, src in ((Wv_s, Wv), (conf_s, conf_w), (Wo_s, Wo)):
                sp.dma_start(dst[:], src).then_inc(const_loaded, 16)
            for dst, src in ((bv_b, bv), (bo_b, bo), (cb_b, conf_b), (wealth_b, wealth)):
                sp.dma_start(dst[:], src.partition_broadcast(P)).then_inc(const_loaded, 16)
            load_w(0, 0)
            load_unit(1, 1)
            load_w(1, 1)
            with sp.Fori(0, (UNITS - 2) // 2) as i:
                for par in range(2):
                    load_unit(i * 2 + 2 + par, par)
                    load_w(i * 2 + 2 + par, par)
            sp.wait_ge(const_made, N_MADE)
            pad_rows = pad_row[:].unsqueeze(1).to_broadcast([P, TB, ROW])
            sp.dma_start(by_expert[E * REGION:E * REGION + TT, :].rearrange("(s p) r -> p s r", s=TB), pad_rows).then_inc(padded, 16)
            sp.wait_ge(pad_at_done, 1)
            for e in range(E):
                at = sp.value_load(pad_at[0:1, e:e + 1], min_val=e * REGION, max_val=e * REGION + NT)
                sp.dma_start(by_expert[bass.ds(at, TT), :].rearrange("(s p) r -> p s r", s=TB), pad_rows).then_inc(padded, 16)
            sp.wait_ge(padded, 16 * (E + 1))
            sp.wait_ge(table, ROWS_AT)

            def load_tile(i, k):
                at = sp.value_load(row_at[0:1, bass.ds(i, 1)], min_val=0, max_val=E * REGION)
                if at_least(i, 4):
                    sp.wait_ge(y_to_done, 2 * (i - 3))
                    sp.wait_ge(xgT_ps, i - 3)
                sp.wait_ge(dispatched, 16 * NB * TOP)
                sp.dma_start(xg[:, k], by_expert[bass.ds(at, TT), :].rearrange("(s p) r -> p s r", s=TB)).then_inc(xg_loaded[k], 16)

            tiles(sp, load_tile)

            for k in range(4):
                sp.wait_ge(y_stored[k], 16 * TB * ((TILES - k + 3) // 4))
            back = by_token.rearrange("(u b t s) d -> u t b s d", u=UNITS, b=UB, s=TOP)
            for u in range(UNITS):
                sp.dma_start(y_back[u % 2][:, u // 2], back[u]).then_inc(y_loaded[u], 16)
            for u in range(UNITS):
                sp.wait_ge(out_done, u + 1)
                sp.dma_start(out_tok[:, bass.ds(u * UB, UB), :], x_all[:, bass.ds(u * UB, UB), :]).then_inc(stored, 16)
            sp.wait_ge(stored, 16 * UNITS)


        @block.gpsimd
        def _(pool):
            n_made = [0]

            def made(ins):
                ins.then_inc(const_made, 1)
                n_made[0] += 1
                pool.wait_ge(const_made, n_made[0])

            def rstd(mv_done, mv, ve, nm, ve_done, rs, rs_done, shift, shift_done, u):
                pool.wait_ge(mv_done, UB * (u + 1))
                pool.tensor_tensor(nm[:], zero[:], mv[:, :, 0], ALU.subtract).then_inc(ve_done, 1)
                pool.tensor_tensor(ve[:], mv[:, :, 1], eps[:], ALU.add).then_inc(ve_done, 1)
                pool.wait_ge(ve_done, 2 * u + 2)
                pool.tensor_tensor(rs[:], ve[:], minus_half[:], ALU.pow).then_inc(rs_done, 1)
                pool.wait_ge(rs_done, u + 1)
                pool.tensor_tensor(shift[:], nm[:], rs[:], ALU.mult).then_inc(shift_done, 1)

            def front(u):
                rstd(mv1_done, mv1, ve1, nm1, ve1_done, rstd1, rstd1_done, shift1, shift1_done, u)

            def front_low(u, par, m):
                dst, src, hi = ((k_lo, k_scaled, k_hi), (q_lo[par], q_scaled, q_hi[par]))[m]
                if m == 0 and not first(u):
                    pool.wait_ge(kmask_lo_done, 4 * u)
                pool.wait_ge(qkscaled_done, 2 * u + m + 1)
                pool.wait_ge(qkhi_done, 2 * u + m + 1)
                pool.tensor_tensor(dst[:], src[:], hi[:], ALU.subtract).then_inc(qklo_done, 1)

            def front_bias(u):
                pool.wait_ge(xhat_done, UB * (u + 1))
                xu = x_all[:, bass.ds(u * UB, UB), :]
                pool.tensor_tensor(xu, xu, bo_b[:].unsqueeze(1).to_broadcast([P, UB, P]), ALU.add).then_inc(xb_done, 1)

            def tail(u):
                rstd(mv2_done, mv2, ve2, nm2, ve2_done, rstd2, rstd2_done, shift2, shift2_done, u)

            def tail_rows(u, par):
                pool.wait_ge(row_hi_done, u + 1)
                for s in range(TOP):
                    pool.tensor_tensor(row_halves[:, :, s, D:2 * D], x2hat[par][:], row_halves[:, :, s, 0:D], ALU.subtract).then_inc(row_lo_done, 1)
                if not first(u):
                    pool.wait_ge(id_next, u)
                pool.tensor_tensor(token_rows[:, :, :, D + 1], pair_id[:], unit_start[:], ALU.add).then_inc(row_id_done, 1)

            def dispatch(u, batches):
                if 0 in batches:
                    pool.wait_ge(row_lo_done, TOP * (u + 1))
                    pool.wait_ge(weights_done, TOP * (u + 1))
                    pool.wait_ge(rows_to_done, u + 1)
                    pool.wait_ge(row_id_done, u + 1)
                    pool.tensor_tensor(unit_start[:], unit_start[:], unit_ids[:], ALU.add).then_inc(id_next, 1)
                for b in batches:
                    for s in range(TOP):
                        pool.indirect_dma_start(by_expert, bass.IndirectOffsetOnAxis(ap=rows_to[:, s, b:b + 1], axis=0),
                                                token_rows[:, b, s, :], None).then_inc(dispatched, 16)

            def body(u, par):
                if not last(u):
                    front(u + 1)
                if not first(u):
                    tail(u - 1)
                if not (isinstance(u, int) and u < 2):
                    dispatch(u - 2, range(UB // 2))
                if not last(u):
                    front_low(u + 1, 1 - par, 0)
                if not (isinstance(u, int) and u < 2):
                    dispatch(u - 2, range(UB // 2, UB))
                if not last(u):
                    front_low(u + 1, 1 - par, 1)
                    front_bias(u + 1)
                if not first(u):
                    tail_rows(u - 1, 1 - par)

            made(pool.memset(ones[:], 1.0))
            made(pool.affine_select(ident[:], ones[:], [[1, P]], ALU.is_equal, 0.0, base=0, channel_multiplier=-1))
            made(pool.memset(minus_half[:], -0.5))
            made(pool.memset(eps[:], EPS))
            made(pool.memset(zero[:], 0.0))
            front(0)
            made(pool.memset(causal[:], 1.0 / (KSCALE * KSCALE)))
            for half in range(2):
                rows = slice(half * CH, half * CH + CH)
                made(pool.affine_select(causal[rows, :], causal[rows, :], [[1, CH]], ALU.is_ge, 0.0, base=0, channel_multiplier=-1))
            ones_h = ones[:, 0:H].rearrange("p (r j) -> p r j", r=RG)
            made(pool.affine_select(headsel[:], ones_h, [[-4 * HD, RG], [-HD, 4]], ALU.is_ge, 0.0, base=0, channel_multiplier=1))
            made(pool.affine_select(headsel[:], headsel[:], [[4 * HD, RG], [HD, 4]], ALU.is_ge, 0.0, base=HD - 1, channel_multiplier=-1))
            bd = blockdiag[:].rearrange("p (h k) -> p h k", h=H)
            made(pool.affine_select(bd, ones[:].rearrange("p (h k) -> p h k", h=H), [[-HD, H], [0, HD]], ALU.is_ge, 0.0, base=0, channel_multiplier=1))
            made(pool.affine_select(bd, bd, [[HD, H], [0, HD]], ALU.is_ge, 0.0, base=HD - 1, channel_multiplier=-1))
            made(pool.iota(iota8[:], [[1, E]], base=0, channel_multiplier=0, allow_small_or_imprecise_dtypes=True))
            made(pool.tensor_copy(ident_h[:], ident[:]))
            made(pool.memset(ones_b[:], 1.0))
            made(pool.affine_select(earlier[:], ones_b[:], [[1, P]], ALU.is_gt, 0.0, base=0, channel_multiplier=-1))
            made(pool.iota(region[:], [[REGION, E]], base=0, channel_multiplier=0, allow_small_or_imprecise_dtypes=True))
            made(pool.iota(pair_id[:], [[TOP * L, UB], [1, TOP]], base=0, channel_multiplier=TOP, allow_small_or_imprecise_dtypes=True))
            made(pool.iota(tile_no[:], [[1, SLOTS]], base=0, channel_multiplier=0, allow_small_or_imprecise_dtypes=True))
            made(pool.memset(before[:], 0.0))
            made(pool.memset(unit_ids[:], float(TOP * UT)))
            made(pool.memset(unit_start[:], 0.0))
            made(pool.memset(pad_row[:], 0.0))
            made(pool.memset(pad_row[:, D + 1:D + 2], FAR))
            pool.wait_ge(const_loaded, 16 * N_LOADS)
            front_bias(0)
            front_low(0, 0, 0)
            front_low(0, 0, 1)
            body(0, 0)
            body(1, 1)
            with pool.Fori(1, UNITS // 2 - 1) as i:
                body(i * 2, 0)
                body(i * 2 + 1, 1)
            body(UNITS - 2, 0)
            body(UNITS - 1, 1)
            dispatch(UNITS - 2, range(UB // 2))
            tail(UNITS - 1)
            dispatch(UNITS - 2, range(UB // 2, UB))
            tail_rows(UNITS - 1, (UNITS - 1) % 2)
            dispatch(UNITS - 1, range(UB))

            def tile_step(i, k):
                if at_least(i, 1):
                    pool.wait_ge(y_done, TB * i)
                if before_end(i):
                    pool.wait_ge(xg_loaded[k], 16 * (i // 4) + 16)
                    if at_least(i, 4):
                        pool.wait_ge(y_stored[k], 16 * TB * (i // 4))
                    pool.tensor_tensor(y_scale[:, k, :], xg[:, k, :, D], ones[:, 0:TB], ALU.mult).then_inc(y_to_done, 1)
                    pool.tensor_copy(y_to[:, k, :], xg[:, k, :, D + 1]).then_inc(y_to_done, 1)
                if at_least(i, 1):
                    kk = (k - 1) % 4
                    for s in range(TB):
                        pool.indirect_dma_start(by_token, bass.IndirectOffsetOnAxis(ap=y_to[:, kk, s:s + 1], axis=0),
                                                y_sb[:, kk, s, :], None, bounds_check=NT * TOP - 1,
                                                oob_is_err=False).then_inc(y_stored[kk], 16)

            tiles(pool, tile_step, 1)

        @block.scalar
        def _(act):
            def weights(u, m):
                act.wait_ge(w_ps, 3 * u + m + 1)
                act.activation(w_hi[:, bass.ds(u * (3 * I) + m * I, I)], bank[2 + m % 2][:], ACT.Copy, scale=WSCALE).then_inc(whi_done, 1)

            def norm(dst, u, rs, shift, done):
                for b in range(UB):
                    act.activation(dst[:, b, :], x_all[:, bass.ds(u * UB + b, 1), :].rearrange("p o d -> p (o d)"),
                                   ACT.Identity, bias=shift[:, b:b + 1], scale=rs[:, b:b + 1]).then_inc(done, 1)

            def front_norm(u):
                act.wait_ge(shift1_done, u + 1)
                if not first(u):
                    act.wait_ge(xT_ps, u)
                norm(xhat, u, rstd1, shift1, xhat_done)

            def tail_norm(u, par):
                act.wait_ge(shift2_done, u + 1)
                norm(x2hat[par], u, rstd2, shift2, x2hat_done)

            def front_copy_x(u):
                act.wait_ge(xT_ps, u + 1)
                act.activation(xT[:], bank[0][:], ACT.Copy).then_inc(xT_copied, 1)

            def front_copy_c(u):
                act.wait_ge(cT_ps, u + 1)
                if not first(u):
                    act.wait_ge(v_ps, u)
                act.activation(cT[:], bank[1][:].rearrange("p (c s) -> p c s", s=CH).unsqueeze(2).to_broadcast([P, NCH, 2, CH]),
                               ACT.Copy).then_inc(cT_copied, 1)

            def front_exp(u, m):
                ps, ready, bneg = ((bank[1], k_ps, bk_neg), (bank[0], q_ps, bq_neg))[m]
                act.wait_ge(ready, u + 1)
                act.activation(expn[:, m, :], ps[:], ACT.Relu, bias=bneg[:], scale=-1.0).then_inc(neg_done, 1)
                act.wait_ge(neg_done, 2 * u + m + 1)
                act.activation(expn[:, m, :], expn[:, m, :], ACT.Exp, scale=-1.0).then_inc(exp_done, 1)

            def front_high(u, par, m):
                dst, src = ((k_hi, kT), (q_hi[par], qT[par]))[m]
                act.wait_ge(qk_done, 2 * u + m + 1)
                if m == 0 and not first(u):
                    act.wait_ge(qklo_done, 2 * u - 1)
                act.activation(dst[:], src[:], ACT.Copy, scale=KSCALE).then_inc(qkhi_done, 1)

            def front_scale(u, par, m):
                dst, src = ((k_scaled, kT), (q_scaled, qT[par]))[m]
                act.wait_ge(qk_done, 2 * u + m + 1)
                if not first(u):
                    act.wait_ge(qklo_done, 2 * u + m - 1)
                act.activation(dst[:], src[:], ACT.Copy, scale=KSCALE).then_inc(qkscaled_done, 1)

            def front_keys_high(u, par):
                act.wait_ge(qkhi_done, 2 * u + 1)
                for j in range(4):
                    act.activation(Khi[par][:, :, j, :], k_hi[:].rearrange("p (c s) -> p c s", s=CH), ACT.Copy,
                                   scale=headmask[:, j:j + 1]).then_inc(kmask_hi_done, 1)

            def front_ktok(u):
                act.wait_ge(ktok_ps, u + 1)
                act.activation(Ktok[:].rearrange("p b d -> p (b d)"), bank[0][0:CH, :], ACT.Copy).then_inc(ktok_copied, 1)

            def tail_x2(u, par):
                act.wait_ge(x2T_ps, u + 1)
                act.activation(x2T[:], bank[7][:], ACT.Copy).then_inc(x2T_copied, 1)

            def tail_rows(u, par):
                act.wait_ge(x2hat_done, UB * (u + 1))
                if not first(u):
                    act.wait_ge(dispatched, 16 * UB * TOP * u)
                act.activation(row_halves[:, :, :, 0:D], x2hat[par][:].unsqueeze(2).to_broadcast([P, UB, TOP, D]), ACT.Copy).then_inc(row_hi_done, 1)

            def tail_exp1(u):
                act.wait_ge(lg_done, u + 1)
                act.activation(conf_e[:], conf[:], ACT.Exp, scale=-1.0).then_inc(lg_exp, 1)

            def tail_exp2(u):
                act.wait_ge(vdiff_done, u + 1)
                act.activation(vexp[:], vdiff[:], ACT.Exp).then_inc(vexp_act, 1)

            def body(u, par):
                weights(u, 0)
                if not last(u):
                    front_copy_c(u + 1)
                weights(u, 1)
                if not last(u):
                    front_norm(u + 1)
                    front_copy_x(u + 1)
                if not first(u):
                    tail_norm(u - 1, 1 - par)
                if not last(u):
                    front_exp(u + 1, 0)
                    front_exp(u + 1, 1)
                if not first(u):
                    tail_x2(u - 1, 1 - par)
                if not last(u):
                    front_scale(u + 1, 1 - par, 0)
                    front_high(u + 1, 1 - par, 0)
                    front_scale(u + 1, 1 - par, 1)
                    front_ktok(u + 1)
                    front_high(u + 1, 1 - par, 1)
                if not first(u):
                    tail_exp1(u - 1)
                if not last(u):
                    front_keys_high(u + 1, 1 - par)
                weights(u, 2)
                if not first(u):
                    tail_exp2(u - 1)
                    tail_rows(u - 1, 1 - par)

            front_copy_c(0)
            front_norm(0)
            front_copy_x(0)
            act.wait_ge(const_dve, 5)
            front_exp(0, 0)
            front_exp(0, 1)
            front_high(0, 0, 0)
            front_scale(0, 0, 0)
            front_high(0, 0, 1)
            front_scale(0, 0, 1)
            front_keys_high(0, 0)
            front_ktok(0)
            units(act, body)
            tail_norm(UNITS - 1, (UNITS - 1) % 2)
            tail_x2(UNITS - 1, (UNITS - 1) % 2)
            tail_exp1(UNITS - 1)
            tail_rows(UNITS - 1, (UNITS - 1) % 2)
            tail_exp2(UNITS - 1)

            def results(i, kk):
                act.wait_ge(y_ps, i + 1)
                act.wait_ge(y_to_done, 2 * i + 2)
                if at_least(i, 4):
                    act.wait_ge(y_stored[kk], 16 * TB * (i // 4))
                for s in range(TB):
                    act.activation(y_sb[:, kk, s, :], bank[6 + kk % 2][:, s * P:(s + 1) * P], ACT.Copy,
                                   scale=y_scale[:, kk, s:s + 1]).then_inc(y_done, 1)

            def tile_step(i, k):
                if before_end(i):
                    for q in range(2):
                        act.wait_ge(gate_ps, 2 * i + q + 1)
                        if at_least(i, 1):
                            act.wait_ge(hid_done, 2 * i + q - 1)
                        act.activation(silu[:, q, :], bank[q][:], ACT.Silu, scale=1.0 / WSCALE).then_inc(silu_done, 1)
                        if q == 1:
                            act.wait_ge(hid_done, 2 * i + 1)
                            if at_least(i, 2):
                                act.wait_ge(y_ps, i - 1)
                            act.activation(hid_hi[:, k % 2, 0, :], hid[:, 0, :], ACT.Copy).then_inc(hi_done, 1)
                if at_least(i, 1):
                    results(i - 1, (k - 1) % 4)
                if before_end(i):
                    act.wait_ge(hid_done, 2 * i + 2)
                    act.activation(hid_hi[:, k % 2, 1, :], hid[:, 1, :], ACT.Copy).then_inc(hi_done, 1)

            act.activation(silu_warm[:], bq_one[:], ACT.Silu)
            tiles(act, tile_step, 1)

        @block.vector
        def _(dve):
            def stats(u, st, st_done):
                for b in range(UB):
                    dve.bn_stats(st[:, b, :], x_all[:, bass.ds(u * UB + b, 1), :].rearrange("p o d -> p (o d)")).then_inc(st_done, 1)

            def aggregate(mv, st, mv_done):
                for b in range(UB):
                    dve.bn_aggr(mv[:, b, :], st[:, b, :]).then_inc(mv_done, 1)

            def carry(i):
                dve.memset(carrier[:, i:i + 1], 0.0)

            def front_stats(u, par):
                dve.wait_ge(x_loaded[par], 16 * (u // 2) + 16)
                carry(0)
                stats(u, stats1, stats1_done)

            def front_aggregate(u):
                dve.wait_ge(stats1_done, UB * (u + 1))
                carry(1)
                aggregate(mv1, stats1, mv1_done)

            def tail_stats(u):
                dve.wait_ge(x1_done, u + 1)
                carry(2)
                stats(u, stats2, stats2_done)

            def tail_aggregate(u):
                dve.wait_ge(stats2_done, UB * (u + 1))
                carry(3)
                aggregate(mv2, stats2, mv2_done)

            def elu_k(u, par):
                dve.wait_ge(exp_done, 2 * u + 1)
                dve.scalar_tensor_tensor(kT[:], bank[1][:], bk_one[:], expn[:, 0, :], ALU.add, ALU.max).then_inc(qk_done, 1)

            def elu_q(u, par):
                dve.wait_ge(exp_done, 2 * u + 2)
                dve.scalar_tensor_tensor(qT[par][:], bank[0][:], bq_one[:], expn[:, 1, :], ALU.add, ALU.max).then_inc(qk_done, 1)

            def front_keys_low(u, par):
                dve.wait_ge(qklo_done, 2 * u + 1)
                for j in range(4):
                    dve.tensor_scalar(Klo[par][:, :, j, :], k_lo[:].rearrange("p (c s) -> p c s", s=CH),
                                      headmask[:, j:j + 1], None, ALU.mult).then_inc(kmask_lo_done, 1)

            def front_v(u, par):
                dve.wait_ge(v_ps, u + 1)
                for half in range(2):
                    ps = bank[2 + half]
                    for a in range(2):
                        rows = slice(a * CH, a * CH + CH)
                        cs = slice(half * NCH // 2, (half + 1) * NCH // 2)
                        src = ps[rows, :].rearrange("p (x j a k) -> p x j a k", j=2, a=2, k=HD)[:, :, :, a, :]
                        dst = Vexp[par][rows, cs].rearrange("p c r j (i a k) -> p (c r) j i a k", i=2, a=2)
                        for j in range(2):
                            bvv = bv_b[rows, :].rearrange("p (r j a k) -> p r j a k", r=RG, j=2, a=2)[:, :, j, a, :]
                            dve.tensor_tensor(
                                dst[:, :, j, j, a, :].rearrange("p (c r) k -> p c r k", r=RG),
                                src[:, :, j, :].rearrange("p (c r) k -> p c r k", r=RG),
                                bvv.unsqueeze(1).to_broadcast([CH, NCH // 2, RG, HD]), ALU.add).then_inc(vexp_done, 1)
                    dve.tensor_tensor(Vtok[:, 2 * half:2 * half + 2, :],
                                      ps[0:CH, :].rearrange("p (b c k) -> p b c k", b=2, c=2)[:, :, 0, :],
                                      bv_b[0:CH, :].unsqueeze(1).to_broadcast([CH, 2, P]), ALU.add).then_inc(vexp_done, 1)

            def front_z(u, par):
                if not first(u):
                    dve.wait_ge(o_done, u)
                for b in range(UB):
                    cols = slice(b * L, (b + 1) * L)
                    dve.tensor_tensor_scan(Z[:, cols], ones[:], qT[par][:, cols], 0.0, ALU.mult, ALU.add).then_inc(z_done, 1)
                dve.wait_ge(z_done, UB * (u + 1))
                dve.reciprocal(Z[:], Z[:]).then_inc(rz_done, 1)

            def front_state(u, par):
                dve.wait_ge(state_ps, u + 1)
                dve.tensor_tensor(state[par][:], bank[1][:].rearrange("p (b k) -> p b k", b=UB),
                                  blockdiag[:].unsqueeze(1).to_broadcast([P, UB, P]), ALU.mult).then_inc(state_done, 1)

            def mask_scores(u, t):
                dve.wait_ge(scores_ps, NBLK * u + t + 1)
                if t >= 4:
                    dve.wait_ge(av_done, NBLK * u + t - 3)
                elif not first(u):
                    dve.wait_ge(av_done, NBLK * u + t - 3)
                dve.tensor_tensor(Pm[:, t % 4, :].rearrange("p (n t) -> p n t", t=CH),
                                  bank[4 + t % 2][:].rearrange("p (n t) -> p n t", t=CH),
                                  causal[:].unsqueeze(1).to_broadcast([P, UT // CH, CH]), ALU.mult).then_inc(p_done, 1)

            def tail_o(u, par):
                dve.wait_ge(av_done, NBLK * (u + 1))
                dve.wait_ge(rz_done, u + 1)
                dve.tensor_tensor(oT[:], bank[6][:], Z[:], ALU.mult).then_inc(o_done, 1)

            def tail_x1(u):
                dve.wait_ge(ao_ps, u + 1)
                dve.wait_ge(xb_done, u + 1)
                xu = x_all[:, bass.ds(u * UB, UB), :]
                dve.tensor_tensor(xu, bank[7][:].rearrange("p (b d) -> p b d", b=UB), xu, ALU.add).then_inc(x1_done, 1)

            ROUTER = 12

            def tail_bids(u):
                dve.wait_ge(lg_ps, u + 1)
                lg = bank[7][:, 0:UB * E].rearrange("p (b e) -> p b e", b=UB)
                dve.tensor_tensor(conf[:], lg, cb_b[:].unsqueeze(1).to_broadcast([P, UB, E]), ALU.add).then_inc(lg_done, 1)

            def tail_choose(u):
                step = [ROUTER * u]

                def done(ins, wait=True):
                    ins.then_inc(router, 1)
                    step[0] = step[0] + 1
                    if wait:
                        dve.wait_ge(router, step[0])

                dve.wait_ge(lg_exp, u + 1)
                done(dve.tensor_scalar(conf[:], conf_e[:], 1.0, None, ALU.add))
                done(dve.reciprocal(conf_e[:], conf[:]))
                done(dve.tensor_tensor(bids[:], conf_e[:], wealth_b[:].unsqueeze(1).to_broadcast([P, UB, E]), ALU.mult))
                carry(4)
                for b in range(UB):
                    dve.max(top[:, b, :], bids[:, b, :]).then_inc(top_done, 1)
                dve.wait_ge(top_done, UB * (u + 1))
                dve.tensor_tensor(vdiff[:], top[:, :, 1], top[:, :, 0], ALU.subtract).then_inc(vdiff_done, 1)
                for b in range(UB):
                    done(dve.max_index(topi[:, b, :], top[:, b, :], bids[:, b, :]), wait=(b == UB - 1))
                for s in range(TOP):
                    done(dve.tensor_tensor(hot[:, s], iota8[:].unsqueeze(1).to_broadcast([P, UB, E]),
                                           topi[:, :, s:s + 1].to_broadcast([P, UB, E]), ALU.is_equal), wait=(s == 1))
                done(dve.tensor_tensor(chosen[:], hot[:, 0], hot[:, 1], ALU.add))

            def tail_weights(u):
                step = [ROUTER * u + 10]

                def done(ins):
                    ins.then_inc(router, 1)
                    step[0] = step[0] + 1
                    dve.wait_ge(router, step[0])

                dve.wait_ge(vexp_act, u + 1)
                done(dve.tensor_scalar(vdiff[:], vexp[:], 1.0, None, ALU.add))
                done(dve.reciprocal(wts[:], vdiff[:]))
                if not first(u):
                    dve.wait_ge(dispatched, 16 * UB * TOP * u)
                dve.tensor_scalar(token_rows[:, :, 0, D], wts[:], 1.0 / WSCALE, None, ALU.mult).then_inc(weights_done, 1)
                dve.scalar_tensor_tensor(token_rows[:, :, 1, D], wts[:], 1.0 / WSCALE, vexp[:], ALU.mult, ALU.mult).then_inc(weights_done, 1)

            def tail_place(u):
                dve.wait_ge(rank_ps, u + 1)
                dve.tensor_tensor(rank[:], bank[7][:, 64:64 + UB * E].rearrange("p (b e) -> p b e", b=UB),
                                  region[:].unsqueeze(1).to_broadcast([P, UB, E]), ALU.add).then_inc(placing, 1)
                dve.tensor_reduce(chosen_sum[:], chosen[:].rearrange("p b e -> p e b"), AX_X, ALU.add).then_inc(placing, 1)
                dve.wait_ge(placing, 3 * u + 2)
                dve.tensor_tensor(place[:], hot[:], rank[:].unsqueeze(1).to_broadcast([P, TOP, UB, E]), ALU.mult).then_inc(placing, 1)
                dve.tensor_tensor(before[:], before[:], chosen_sum[:], ALU.add).then_inc(before_done, 1)
                dve.wait_ge(placing, 3 * u + 3)
                with nc.allow_low_precision(reason="a row's number is a whole number, exact in any of the types"):
                    dve.tensor_reduce(rows_to[:], place[:], AX_X, ALU.add).then_inc(rows_to_done, 1)

            def weights(u, m):
                dve.wait_ge(whi_done, 3 * u + m + 1)
                cols = bass.ds(u * (3 * I) + m * I, I)
                dve.scalar_tensor_tensor(w_lo[:, cols], bank[2 + m % 2][:], WSCALE, w_hi[:, cols], ALU.mult, ALU.subtract).then_inc(wlo_done, 1)

            def body(u, par):
                if not first(u):
                    tail_o(u - 1, 1 - par)
                if not last(u):
                    front_stats(u + 1, 1 - par)
                mask_scores(u, 1)
                if not last(u):
                    front_aggregate(u + 1)
                weights(u, 0)
                if not first(u):
                    tail_x1(u - 1)
                    tail_stats(u - 1)
                weights(u, 1)
                if not first(u):
                    tail_aggregate(u - 1)
                mask_scores(u, 2)
                front_z(u, par)
                mask_scores(u, 3)
                if not last(u):
                    elu_k(u + 1, 1 - par)
                mask_scores(u, 4)
                if not last(u):
                    elu_q(u + 1, 1 - par)
                    front_v(u + 1, 1 - par)
                mask_scores(u, 5)
                if not first(u):
                    tail_bids(u - 1)
                if not last(u):
                    front_keys_low(u + 1, 1 - par)
                if not first(u):
                    tail_choose(u - 1)
                mask_scores(u, 6)
                mask_scores(u, 7)
                if not last(u):
                    front_state(u + 1, 1 - par)
                weights(u, 2)
                if not first(u):
                    tail_weights(u - 1)
                    tail_place(u - 1)
                if not last(u):
                    mask_scores(u + 1, 0)

            front_stats(0, 0)
            front_aggregate(0)
            dve.wait_ge(qk_loaded, 16 * 4)
            for b_c, b_n, b_1 in ((bk_c, bk_neg, bk_one), (bq_c, bq_neg, bq_one)):
                dve.tensor_scalar(b_n[:], b_c[:], -1.0, None, ALU.mult).then_inc(const_dve, 1)
                dve.tensor_scalar(b_1[:], b_c[:], 1.0, None, ALU.add).then_inc(const_dve, 1)
            for i in range(2):
                dve.memset(Vexp[i][:], 0.0)
            dve.wait_ge(const_made, N_MADE)
            dve.tensor_reduce(headmask[:], headsel[:].rearrange("p r j -> p j r"), AX_X, ALU.add).then_inc(const_dve, 1)
            dve.wait_ge(const_dve, 5)
            elu_k(0, 0)
            elu_q(0, 0)
            front_keys_low(0, 0)
            dve.wait_ge(const_loaded, 16 * N_LOADS)
            front_v(0, 0)
            dve.wait_ge(confT_ps, 1)
            dve.tensor_copy(confT[:], bank[7][:, 0:E]).then_inc(const_dve, 1)
            mask_scores(0, 0)
            front_state(0, 0)
            units(dve, body)
            tail_o(UNITS - 1, (UNITS - 1) % 2)
            tail_x1(UNITS - 1)
            tail_stats(UNITS - 1)
            tail_aggregate(UNITS - 1)
            tail_bids(UNITS - 1)
            tail_choose(UNITS - 1)
            tail_weights(UNITS - 1)
            tail_place(UNITS - 1)

            n_table = [0]

            def entry(ins):
                ins.then_inc(table, 1)
                n_table[0] += 1
                dve.wait_ge(table, n_table[0])

            dve.wait_ge(count_ps, 1)
            entry(dve.tensor_copy(count[:], bank[7][0:1, 96:96 + E]))
            dve.tensor_tensor(pad_at[:], count[:], region[0:1, :], ALU.add).then_inc(pad_at_done, 1)
            entry(dve.tensor_scalar(blocks_u[:], count[:], float(TT - 1), None, ALU.add))
            entry(dve.tensor_scalar(blocks_s[:], blocks_u[:], TT.bit_length() - 1, None, ALU.logical_shift_right))
            entry(dve.tensor_copy(blocks[:], blocks_s[:]))
            entry(dve.tensor_tensor_scan(blocks_to[:], ones[0:1, 0:E], blocks[:], 0.0, ALU.mult, ALU.add))
            entry(dve.tensor_tensor(passed[:], tile_no[:].unsqueeze(2).to_broadcast([1, SLOTS, E]),
                                    blocks_to[:].unsqueeze(1).to_broadcast([1, SLOTS, E]), ALU.is_ge))
            entry(dve.tensor_reduce(tile_expert[:], passed[:], AX_X, ALU.add))
            entry(dve.tensor_tensor(passed_blocks[:], passed[:], blocks[:].unsqueeze(1).to_broadcast([1, SLOTS, E]), ALU.mult))
            entry(dve.tensor_reduce(tile_start[:], passed_blocks[:], AX_X, ALU.add))
            entry(dve.tensor_tensor(tile_start[:], tile_no[:], tile_start[:], ALU.subtract))
            entry(dve.tensor_scalar(tile_start[:], tile_start[:], float(TT), None, ALU.mult))
            entry(dve.scalar_tensor_tensor(tile_row[:], tile_expert[:], float(REGION), tile_start[:], ALU.mult, ALU.add))
            entry(dve.tensor_scalar(row_at[:], tile_row[:], float(E * REGION), None, ALU.min))
            entry(dve.memset(expert_of[:], 0.0))
            entry(dve.tensor_scalar(expert_of[:, 1:1 + SLOTS], tile_expert[:], float(E - 1), None, ALU.min))
            digits = [expert_of[:, k // 4 * 4:k // 4 * 4 + SLOTS].rearrange("o (j k) -> o j k", k=4)[:, :, k % 4] for k in range(5)]
            entry(dve.scalar_tensor_tensor(packed[:], digits[4], float(E), digits[3], ALU.mult, ALU.add))
            for k in (2, 1):
                entry(dve.scalar_tensor_tensor(packed[:], packed[:], float(E), digits[k], ALU.mult, ALU.add))
            entry(dve.scalar_tensor_tensor(experts_at[:], packed[:], float(E), digits[0], ALU.mult, ALU.add))
            assert n_table[0] == TABLE, n_table[0]

            def copy_T(i, k):
                dve.wait_ge(xgT_ps, i + 1)
                if at_least(i, 2):
                    dve.wait_ge(up_ps, 2 * (i - 1))
                dve.tensor_copy(xgT[:, k % 2].rearrange("p h t -> p (h t)"), bank[4 + k % 2][:, 0:TT].bitcast(F16)).then_inc(xgT_copied, 1)

            def hidden(i, k, q):
                dve.wait_ge(silu_done, 2 * i + q + 1)
                dve.wait_ge(up_ps, 2 * i + q + 1)
                if at_least(i, 1):
                    dve.wait_ge(lo_done, 2 * i + q - 1)
                dve.scalar_tensor_tensor(hid[:, q, :], bank[2 + q][:], 1.0 / WSCALE, silu[:, q, :],
                                         ALU.mult, ALU.mult).then_inc(hid_done, 1)

            def low(i, k, q):
                dve.wait_ge(hi_done, 2 * i + q + 1)
                dve.tensor_tensor(hid_lo[:, k % 2, q, :], hid[:, q, :], hid_hi[:, k % 2, q, :], ALU.subtract).then_inc(lo_done, 1)

            def tile_step(i, k):
                hidden(i, k, 0)
                if before_end(i, TILES - 2):
                    copy_T(i + 2, k + 2)
                hidden(i, k, 1)
                low(i, k, 0)
                low(i, k, 1)

            copy_T(0, 0)
            copy_T(1, 1)
            tiles(dve, tile_step)

            for u in range(UNITS):
                dve.wait_ge(y_loaded[u], 16)
                xu = x_all[:, u * UB:(u + 1) * UB, :]
                dve.tensor_tensor(xu, xu, y_back[u % 2][:, u // 2, :, 0, :], ALU.add).then_inc(sum_done, 1)
                dve.wait_ge(sum_done, u + 1)
                dve.tensor_tensor(xu, xu, y_back[u % 2][:, u // 2, :, 1, :], ALU.add).then_inc(out_done, 1)

        @block.tensor
        def _(pe):
            def weights(u, par, m):
                if m == 0:
                    if first(u):
                        pe.wait_ge(vexp_done, 10)
                    pe.wait_ge(w_loaded[par], 48 * (u // 2) + 48)
                    if not first(u):
                        pe.wait_ge(wlo_done, 3 * u)
                elif m == 1:
                    pe.wait_ge(vexp_done, 10 * (u + 1))
                elif last(u):
                    pe.wait_ge(wlo_done, 3 * u + 1)
                else:
                    pe.wait_ge(vexp_done, 10 * (u + 2))
                for c in range(IC):
                    ins = pe.transpose(bank[2 + m % 2][:, c * P:(c + 1) * P], w_raw[par][:, m, c * P:(c + 1) * P], ident[:])
                ins.then_inc(w_ps, 1)

            def front_transpose_x(u):
                pe.wait_ge(xhat_done, UB * (u + 1))
                if not first(u):
                    pe.wait_ge(ktok_copied, u)
                for b in range(UB):
                    ins = pe.transpose(bank[0][:, b * L:(b + 1) * L], xhat[:, b, :], ident[:])
                ins.then_inc(xT_ps, 1)

            def front_transpose_c(u, par):
                pe.wait_ge(ctx_loaded[par], 16 * (u // 2) + 16)
                if not first(u):
                    pe.wait_ge(state_done, u)
                for b in range(UB):
                    ins = pe.transpose(bank[1][:, b * L:(b + 1) * L], ctx_s[par][:, b, :], ident[:])
                ins.then_inc(cT_ps, 1)

            def front_project_k(u):
                pe.wait_ge(cT_copied, u + 1)
                pe.matmul(bank[1][:], Wk_s[:], cT[:, :, 0, :], start=True, stop=True).then_inc(k_ps, 1)

            def front_project_q(u):
                pe.wait_ge(xT_copied, u + 1)
                pe.matmul(bank[0][:], Wq_s[:], xT[:], start=True, stop=True).then_inc(q_ps, 1)

            def front_values(u):
                pe.wait_ge(cT_copied, u + 1)
                if not first(u):
                    pe.wait_ge(wlo_done, 3 * u - 1)
                for c in range(NCH):
                    ins = pe.matmul(bank[2 + c // 4][:, (c % 4) * P:(c % 4 + 1) * P], cT[:, c, :, :], Wv_s[:], start=True, stop=True)
                ins.then_inc(v_ps, 1)

            def front_ktok(u):
                pe.wait_ge(qk_done, 2 * u + 2)
                for b in range(UB):
                    ins = pe.transpose(bank[0][:, b * P:(b + 1) * P], kT[:, b * L:(b + 1) * L], ident[:])
                ins.then_inc(ktok_ps, 1)

            def front_state(u):
                pe.wait_ge(ktok_copied, u + 1)
                pe.wait_ge(vexp_done, 10 * (u + 1))
                for b in range(UB):
                    ins = pe.matmul(bank[1][:, b * P:(b + 1) * P], Ktok[:, b, :], Vtok[:, b, :], start=True, stop=True)
                ins.then_inc(state_ps, 1)

            def scores(u, par, t):
                bb, r = t // RG, t % RG
                rows = slice(32 * r, 32 * r + 32)
                if t == 0:
                    pe.wait_ge(kmask_hi_done, 4 * (u + 1))
                    pe.wait_ge(kmask_lo_done, 4 * (u + 1))
                    pe.wait_ge(qklo_done, 2 * (u + 1))
                if t >= 2:
                    pe.wait_ge(p_done, NBLK * u + t - 1)
                elif not first(u):
                    pe.wait_ge(p_done, NBLK * u + t - 1)
                for n in range(4):
                    c = bb * 4 + n
                    q_h, q_l = q_hi[par][rows, c * CH:(c + 1) * CH], q_lo[par][rows, c * CH:(c + 1) * CH]
                    for j in range(2):
                        ps = bank[4 + t % 2][:, (n * 2 + j) * CH:(n * 2 + j + 1) * CH]
                        k_h, k_l = Khi[par][rows, c, 2 * j:2 * j + 2, :], Klo[par][rows, c, 2 * j:2 * j + 2, :]
                        pe.matmul(ps, k_h, q_h, start=(n == 0 and j == 0), stop=False, skip_group_check=True)
                        pe.matmul(ps, k_h, q_l, start=False, stop=False, skip_group_check=True)
                        ins = pe.matmul(ps, k_l, q_h, start=False, stop=True, skip_group_check=True)
                ins.then_inc(scores_ps, 1)

            def values(u, par, t):
                bb, r = t // RG, t % RG
                rows = slice(32 * r, 32 * r + 32)
                if t == 0:
                    pe.wait_ge(state_done, u + 1)
                    if not first(u):
                        pe.wait_ge(o_done, u)
                    for b in range(UB):
                        pe.matmul(bank[6][:, b * L + CH:(b + 1) * L], state[par][:, b, :], qT[par][:, b * L + CH:(b + 1) * L],
                                  start=(b == 0), stop=False, skip_group_check=True)
                pe.wait_ge(p_done, NBLK * u + t + 1)
                for n in range(4):
                    c = bb * 4 + n
                    for j in range(2):
                        ins = pe.matmul(bank[6][rows, c * CH:(c + 1) * CH], Vexp[par][:, c, r, j, :],
                                        Pm[:, t % 4, (n * 2 + j) * CH:(n * 2 + j + 1) * CH],
                                        start=False, stop=(j == 1), skip_group_check=True)
                ins.then_inc(av_done, 1)

            def tail_out(u):
                pe.wait_ge(o_done, u + 1)
                if not first(u):
                    pe.wait_ge(rows_to_done, u)
                for b in range(UB):
                    ins = pe.matmul(bank[7][:, b * P:(b + 1) * P], oT[:, b * L:(b + 1) * L], Wo_s[:], start=True, stop=True)
                ins.then_inc(ao_ps, 1)

            def tail_x2(u, par):
                pe.wait_ge(x2hat_done, UB * (u + 1))
                for b in range(UB):
                    ins = pe.transpose(bank[7][:, b * L:(b + 1) * L], x2hat[par][:, b, :], ident[:])
                ins.then_inc(x2T_ps, 1)

            def tail_logits(u):
                pe.wait_ge(x2T_copied, u + 1)
                for b in range(UB):
                    ins = pe.matmul(bank[7][:, b * E:(b + 1) * E], x2T[:, b * L:(b + 1) * L], confT[:], start=True, stop=True)
                ins.then_inc(lg_ps, 1)

            def tail_rank(u):
                pe.wait_ge(router, 12 * u + 10)
                if not first(u):
                    pe.wait_ge(before_done, u)
                ps = bank[7][:, 64:64 + UB * E]
                pe.matmul(ps, earlier[:], chosen[:].rearrange("p b e -> p (b e)"), start=True, stop=False, skip_group_check=True)
                for b in range(UB - 1):
                    pe.matmul(ps[:, (b + 1) * E:].rearrange("p (n e) -> p n e", e=E), ones_b[:],
                              chosen[:, b:b + 1, :].to_broadcast([P, UB - 1 - b, E]), start=False, stop=False, skip_group_check=True)
                pe.matmul(ps.rearrange("p (b e) -> p b e", b=UB), ones_b[:], before[:].unsqueeze(1).to_broadcast([P, UB, E]),
                          start=False, stop=True, skip_group_check=True).then_inc(rank_ps, 1)

            def body(u, par):
                if not last(u):
                    front_transpose_c(u + 1, 1 - par)
                weights(u, par, 0)
                if not first(u):
                    tail_out(u - 1)
                weights(u, par, 1)
                scores(u, par, 2)
                values(u, par, 0)
                if not last(u):
                    front_transpose_x(u + 1)
                scores(u, par, 3)
                if not last(u):
                    front_project_k(u + 1)
                    front_project_q(u + 1)
                scores(u, par, 4)
                if not first(u):
                    tail_x2(u - 1, 1 - par)
                if not last(u):
                    front_values(u + 1)
                values(u, par, 1)
                values(u, par, 2)
                if not first(u):
                    tail_logits(u - 1)
                if not last(u):
                    front_ktok(u + 1)
                scores(u, par, 5)
                values(u, par, 3)
                scores(u, par, 6)
                values(u, par, 4)
                weights(u, par, 2)
                scores(u, par, 7)
                if not last(u):
                    front_state(u + 1)
                    scores(u + 1, 1 - par, 0)
                if not first(u):
                    tail_rank(u - 1)
                values(u, par, 5)
                if not last(u):
                    scores(u + 1, 1 - par, 1)
                values(u, par, 6)
                values(u, par, 7)

            pe.wait_ge(const_made, 2)
            front_transpose_c(0, 0)
            pe.wait_ge(qk_loaded, 16 * 4)
            front_project_k(0)
            front_transpose_x(0)
            front_project_q(0)
            pe.wait_ge(const_loaded, 16 * N_LOADS)
            front_values(0)
            front_ktok(0)
            pe.transpose(bank[7][:, 0:E], conf_s[:], ident[0:E, 0:E]).then_inc(confT_ps, 1)
            pe.wait_ge(const_made, N_MADE)
            scores(0, 0, 0)
            scores(0, 0, 1)
            front_state(0)
            pe.wait_ge(const_dve, 6)
            units(pe, body)
            tail_out(UNITS - 1)
            tail_x2(UNITS - 1, (UNITS - 1) % 2)
            tail_logits(UNITS - 1)
            tail_rank(UNITS - 1)
            pe.wait_ge(before_done, UNITS)
            pe.matmul(bank[7][:, 96:96 + E], ones_b[:], before[:], start=True, stop=True).then_inc(count_ps, 1)

            def transposes(i, k):
                pe.wait_ge(xg_loaded[k % 4], 16 * (i // 4) + 16)
                if at_least(i, 2):
                    pe.wait_ge(xgT_copied, i - 1)
                for half in range(2):
                    for s in range(TB):
                        at = half * TB + s
                        ins = pe.transpose(bank[4 + k % 2][:, at * (P // 2):(at + 1) * (P // 2)].bitcast(F16),
                                           xg_halves[:, k % 4, s, half * P:(half + 1) * P], ident_h[:])
                ins.then_inc(xgT_ps, 1)

            def gate_up(i, k, col):
                pe.wait_ge(xgT_copied, i + 1)
                x_hi, x_lo = xgT[:, k % 2, 0, :], xgT[:, k % 2, 1, :]
                for q in range(2):
                    if at_least(i, 1):
                        pe.wait_ge(hid_done, 2 * i + q - 1)
                    for m, ready in ((0, gate_ps), (1, up_ps)):
                        for c in range(HC):
                            ps = bank[2 * m + q][:, c * TT:(c + 1) * TT]
                            w = bass.ds(col + (m * I + (q * HC + c) * P), P)
                            pe.matmul(ps, w_hi[:, w], x_hi, start=(c == 0), stop=False, skip_group_check=True)
                            pe.matmul(ps, w_hi[:, w], x_lo, start=False, stop=False, skip_group_check=True)
                            ins = pe.matmul(ps, w_lo[:, w], x_hi, start=False, stop=True, skip_group_check=True)
                        ins.then_inc(ready, 1)

            def down(i, k, col):
                pe.wait_ge(lo_done, 2 * i + 2)
                if at_least(i, 2):
                    pe.wait_ge(y_done, TB * (i - 1))
                for c in range(IC):
                    w = bass.ds(col + (2 * I + c * P), P)
                    for s in range(TB):
                        ps = bank[6 + k % 2][:, s * P:(s + 1) * P]
                        q, h = c // HC, slice((c % HC) * TT + s * P, (c % HC) * TT + (s + 1) * P)
                        pe.matmul(ps, hid_hi[:, k % 2, q, h], w_hi[:, w], start=(c == 0 and s == 0), stop=False, skip_group_check=True)
                        pe.matmul(ps, hid_hi[:, k % 2, q, h], w_lo[:, w], start=False, stop=False, skip_group_check=True)
                        ins = pe.matmul(ps, hid_lo[:, k % 2, q, h], w_hi[:, w], start=False, stop=(c == IC - 1), skip_group_check=True)
                ins.then_inc(y_ps, 1)

            def load_cols(i, n):
                _, words = nc.values_load_multi_w_load_instructions(
                    experts_at[0:1, bass.ds(i, -(-n // 4))], engines=(mybir.EngineType.PE,), min_val=0, max_val=E ** 5 - 1)
                cols = []
                for w, word in enumerate(words):
                    for k in range(min(w, 1), 5):
                        expert = word // E ** k % E if k < 4 else word // E ** k
                        cols.append(nc.snap(expert * (3 * I), engines=(mybir.EngineType.PE,), min_val=0, max_val=(E - 1) * 3 * I))
                return cols

            def tile_steps(i0, n, at):
                cols = load_cols(at, n)
                for k in range(n):
                    gate_up(i0 + k, k % 4, cols[1 + k])
                    if before_end(i0 + k, TILES - 2):
                        transposes(i0 + k + 2, (k + 2) % 4)
                    if at_least(i0 + k, 1):
                        down(i0 + k - 1, (k - 1) % 4, cols[k])
                return cols[n]

            TURN = 8
            assert SLOTS % TURN == 0
            pe.wait_ge(wlo_done, 3 * E)
            pe.wait_ge(table, TABLE)
            transposes(0, 0)
            transposes(1, 1)
            tile_steps(0, 4, 0)
            with pe.Fori(0, SLOTS // TURN - 1) as n:
                tile_steps(n * TURN + 4, TURN, n * (TURN // 4) + 1)
            col = tile_steps(SLOTS - 4, TILES - (SLOTS - 4), SLOTS // 4 - 1)
            down(TILES - 1, (TILES - 1) % 4, col)


_INS = ['x', 'ctx_1024', 'L0_xattn_Wq', 'L0_xattn_bq', 'L0_xattn_Wk', 'L0_xattn_bk', 'L0_xattn_Wv', 'L0_xattn_bv',
        'L0_xattn_Wo', 'L0_xattn_bo', 'L0_ffn_conf_w', 'L0_ffn_conf_b', 'L0_ffn_gate_w', 'L0_ffn_up_w',
        'L0_ffn_down_w', 'L0_ffn_wealth']


def kernel(**inputs):
    import numpy as _np
    import concourse.bacc as _bacc
    from concourse import mybir as _mybir
    from concourse.bass_utils import run_bass_kernel_spmd as _run

    nc = _bacc.Bacc("TRN2", target_bir_lowering=False, num_devices=1)
    arrays, args = {}, []
    for name in _INS:
        a = _np.ascontiguousarray(inputs[name])
        arrays[f"in_{name}_dram"] = a
        args.append(nc.dram_tensor(f"in_{name}_dram", a.shape, _mybir.dt.from_np(a.dtype), kind="ExternalInput").ap())
    shape = arrays["in_x_dram"].shape
    args.append(nc.dram_tensor("out_dram", shape, _mybir.dt.float32, kind="ExternalOutput").ap())
    attention_moe_kernel(nc, *args)
    r = _run(nc, [arrays], core_ids=[0])
    return r.results[0]["out_dram"]
```
